# Optimizing a Trainium2 kernel written in Bass

```python
import numpy as np
import jax
import jax.numpy as jnp

def _softmax(x, axis=-1):
    return jax.nn.softmax(x, axis=axis)

def _gelu(x):
    return jax.nn.gelu(x, approximate=True)

def _silu(x):
    return jax.nn.silu(x)

def _sigmoid(x):
    return jax.nn.sigmoid(x)

def _layernorm(x, axis=-1, eps=1e-05):
    m = jnp.mean(x, axis=axis, keepdims=True)
    v = jnp.var(x, axis=axis, keepdims=True)
    return (x - m) / jnp.sqrt(v + eps)

def _scatter_add(tgt, idx, src, axis=0):
    return tgt.at[idx].add(src)

def _segment_sum(src, seg, n):
    return jax.ops.segment_sum(src, seg, n)
kernel_name = 'mk_adaln_ffn_d1_seqx_r8_0397f0'

def setup_inputs(seed: int=0):
    np.random.seed(seed)
    _w = jnp.asarray

    def _rec_inputs():
        import jax
        import jax.numpy as jnp
        _rk = jax.random.key(seed)
        x = -0.000125 + 0.9999 * jax.random.normal(jax.random.fold_in(_rk, 1), (64, 32, 512), jnp.float32)
        _lenS = 32 - jax.random.randint(jax.random.fold_in(_rk, 7), (64,), 0, max(1, 32 // 4) + 1, jnp.int32)
        _lenS2 = 32 - jax.random.randint(jax.random.fold_in(_rk, 8), (64,), 0, max(1, 32 // 4) + 1, jnp.int32)
        cond_128 = 0.0061147 + 1.02565 * jax.random.normal(jax.random.fold_in(_rk, 11), (64, 128), jnp.float32)
        return (x, cond_128)
    x, cond_128 = _rec_inputs()

    def _L0_cond_setup():
        import jax, jax.numpy as jnp
        import numpy as np
        K = 8
        T = 1.0
        D_EMBD = 128
        IN_C = 32
        OUT_C = 32
        BS = 32
        H = 512
        HID = 128
        key = jax.random.key(seed)
        ks = jax.random.split(key, 10)
        s = lambda fan_in: 1.0 / np.sqrt(fan_in)
        return {'x': jax.random.normal(ks[0], (BS, IN_C, H), dtype=jnp.float32), 'embedding': jax.random.normal(ks[1], (BS, D_EMBD), dtype=jnp.float32), 'W0': jax.random.normal(ks[2], (D_EMBD, HID), dtype=jnp.float32) * s(D_EMBD), 'b0': jnp.zeros((HID,), dtype=jnp.float32), 'W1': jax.random.normal(ks[3], (HID, HID), dtype=jnp.float32) * s(HID), 'b1': jnp.zeros((HID,), dtype=jnp.float32), 'W2': jax.random.normal(ks[4], (HID, K), dtype=jnp.float32) * s(HID), 'b2': jnp.zeros((K,), dtype=jnp.float32), 'weight': jax.random.normal(ks[5], (K, OUT_C, IN_C, 1), dtype=jnp.float32) * s(IN_C), 'bias_k': jax.random.normal(ks[6], (K, OUT_C), dtype=jnp.float32) * 0.1}
    _L0_cond_all = _L0_cond_setup()
    _L0_cond_in = {k: v for k, v in _L0_cond_all.items() if k in ('W0', 'b0', 'W1', 'b1', 'W2', 'b2', 'weight', 'bias_k')}
    del _L0_cond_all

    def _L0_ffn_setup():
        import jax, jax.numpy as jnp
        import numpy as np
        DIM = 512
        INTER = 128
        E = 16
        GROUPS = 4
        LIM = 2
        K = 2
        SHARED_INTER = 2 * INTER
        SCALE = 1.0
        key = jax.random.key(seed)
        ks = jax.random.split(key, 16)

        def n(k, shape, s=0.02):
            return jax.random.normal(k, shape, jnp.float32) * s
        return {'x': jax.random.normal(ks[0], (1, 256, DIM), jnp.float32), 'router_w': n(ks[1], (DIM, E)), 'router_b': n(ks[2], (E,)), 'router_bias': n(ks[3], (E,), 1.0), 'ew1': n(ks[4], (E, DIM, INTER)), 'eb1': n(ks[5], (E, INTER)), 'ew2': n(ks[6], (E, DIM, INTER)), 'eb2': n(ks[7], (E, INTER)), 'ew3': n(ks[8], (E, INTER, DIM)), 'eb3': n(ks[9], (E, DIM)), 'sw1': n(ks[10], (DIM, SHARED_INTER)), 'sb1': n(ks[11], (SHARED_INTER,)), 'sw2': n(ks[12], (DIM, SHARED_INTER)), 'sb2': n(ks[13], (SHARED_INTER,)), 'sw3': n(ks[14], (SHARED_INTER, DIM)), 'sb3': n(ks[15], (DIM,))}
    _L0_ffn_all = _L0_ffn_setup()
    _L0_ffn_in = {k: v for k, v in _L0_ffn_all.items() if k in ('router_w', 'router_b', 'router_bias', 'ew1', 'eb1', 'ew2', 'eb2', 'ew3', 'eb3', 'sw1', 'sb1', 'sw2', 'sb2', 'sw3', 'sb3')}
    del _L0_ffn_all
    return {'x': x, 'cond_128': cond_128, 'L0_cond_W0': _L0_cond_in['W0'], 'L0_cond_b0': _L0_cond_in['b0'], 'L0_cond_W1': _L0_cond_in['W1'], 'L0_cond_b1': _L0_cond_in['b1'], 'L0_cond_W2': _L0_cond_in['W2'], 'L0_cond_b2': _L0_cond_in['b2'], 'L0_cond_weight': _L0_cond_in['weight'], 'L0_cond_bias_k': _L0_cond_in['bias_k'], 'L0_ffn_router_w': _L0_ffn_in['router_w'], 'L0_ffn_router_b': _L0_ffn_in['router_b'], 'L0_ffn_router_bias': _L0_ffn_in['router_bias'], 'L0_ffn_ew1': _L0_ffn_in['ew1'], 'L0_ffn_eb1': _L0_ffn_in['eb1'], 'L0_ffn_ew2': _L0_ffn_in['ew2'], 'L0_ffn_eb2': _L0_ffn_in['eb2'], 'L0_ffn_ew3': _L0_ffn_in['ew3'], 'L0_ffn_eb3': _L0_ffn_in['eb3'], 'L0_ffn_sw1': _L0_ffn_in['sw1'], 'L0_ffn_sb1': _L0_ffn_in['sb1'], 'L0_ffn_sw2': _L0_ffn_in['sw2'], 'L0_ffn_sb2': _L0_ffn_in['sb2'], 'L0_ffn_sw3': _L0_ffn_in['sw3'], 'L0_ffn_sb3': _L0_ffn_in['sb3']}

def reference(x, cond_128, L0_cond_W0, L0_cond_b0, L0_cond_W1, L0_cond_b1, L0_cond_W2, L0_cond_b2, L0_cond_weight, L0_cond_bias_k, L0_ffn_router_w, L0_ffn_router_b, L0_ffn_router_bias, L0_ffn_ew1, L0_ffn_eb1, L0_ffn_ew2, L0_ffn_eb2, L0_ffn_ew3, L0_ffn_eb3, L0_ffn_sw1, L0_ffn_sb1, L0_ffn_sw2, L0_ffn_sb2, L0_ffn_sw3, L0_ffn_sb3):
    import jax
    import jax.numpy as jnp

    def _L0_cond_ref(x, embedding, W0, b0, W1, b1, W2, b2, weight, bias_k):
        import jax, jax.numpy as jnp
        import numpy as np
        K = 8
        T = 1.0
        D_EMBD = 128
        IN_C = 32
        OUT_C = 32
        BS = 32
        H = 512
        HID = 128
        h = jax.nn.gelu(embedding @ W0 + b0, approximate=False)
        h = jax.nn.gelu(h @ W1 + b1, approximate=False)
        att = jax.nn.softmax((h @ W2 + b2) / T, axis=-1)
        agg_w = jnp.einsum('bk,koi->boi', att, weight[..., 0])
        agg_b = att @ bias_k
        out = jnp.einsum('boi,bih->boh', agg_w, x) + agg_b[:, :, None]
        return out

    def _L0_ffn_ref(x, router_w, router_b, router_bias, ew1, eb1, ew2, eb2, ew3, eb3, sw1, sb1, sw2, sb2, sw3, sb3):
        import jax, jax.numpy as jnp
        import numpy as np
        DIM = 512
        INTER = 128
        E = 16
        GROUPS = 4
        LIM = 2
        K = 2
        SHARED_INTER = 2 * INTER
        SCALE = 1.0
        shape = x.shape
        xt = x.reshape(-1, DIM)
        T = xt.shape[0]
        logits = xt @ router_w + router_b
        scores = jax.nn.softmax(logits.astype(jnp.float32), axis=-1) + router_bias
        g = scores.reshape(T, GROUPS, E // GROUPS)
        _, gidx = jax.lax.top_k(g.max(axis=-1), LIM)
        keep = jnp.zeros((T, GROUPS), bool).at[jnp.arange(T)[:, None], gidx].set(True)
        masked = jnp.where(keep[:, :, None], g, -jnp.inf).reshape(T, E)
        _, idx = jax.lax.top_k(masked, K)
        vals = (jnp.take_along_axis(scores, idx, axis=1) * SCALE).astype(x.dtype)
        gate = jnp.zeros((T, E), x.dtype).at[jnp.arange(T)[:, None], idx].add(vals)

        def step(y, p):
            w1, b1, w2, b2, w3, b3, ge = p
            h = jax.nn.silu(xt @ w1 + b1) * (xt @ w2 + b2)
            return (y + ge[:, None] * (h @ w3 + b3), None)
        y, _ = jax.lax.scan(step, jnp.zeros_like(xt), (ew1, eb1, ew2, eb2, ew3, eb3, gate.T))
        z = jax.nn.silu(xt @ sw1 + sb1) * (xt @ sw2 + sb2) @ sw3 + sb3
        return (y + z).reshape(shape)
    x = x + _L0_ffn_ref(_L0_cond_ref(x, cond_128, L0_cond_W0, L0_cond_b0, L0_cond_W1, L0_cond_b1, L0_cond_W2, L0_cond_b2, L0_cond_weight, L0_cond_bias_k), L0_ffn_router_w, L0_ffn_router_b, L0_ffn_router_bias, L0_ffn_ew1, L0_ffn_eb1, L0_ffn_ew2, L0_ffn_eb2, L0_ffn_ew3, L0_ffn_eb3, L0_ffn_sw1, L0_ffn_sb1, L0_ffn_sw2, L0_ffn_sb2, L0_ffn_sw3, L0_ffn_sb3)
    return x

_drawn_inputs = setup_inputs


def setup_inputs(seed=0):
    import zlib

    import numpy as np

    out = dict(_drawn_inputs(seed))
    spreads = {'L0_cond_b0': (0.0, 2.0), 'L0_cond_b1': (0.0, 0.8), 'L0_cond_b2': (0.0, 2.0)}
    factors = {'cond_128': 8.0,
     'L0_cond_W0': 8.0,
     'L0_cond_W1': 8.0,
     'L0_cond_W2': 8.0,
     'L0_cond_weight': 5.295,
     'L0_cond_bias_k': 8.0,
     'L0_ffn_router_w': 8.0,
     'L0_ffn_router_b': 8.0,
     'L0_ffn_ew1': 5.887,
     'L0_ffn_eb1': 64.0,
     'L0_ffn_ew2': 5.844,
     'L0_ffn_eb2': 64.0,
     'L0_ffn_ew3': 5.807,
     'L0_ffn_sw1': 8.0,
     'L0_ffn_sb1': 64.0,
     'L0_ffn_sw2': 8.0,
     'L0_ffn_sb2': 64.0,
     'L0_ffn_sw3': 8.0,
     'L0_ffn_sb3': 22.784,
     'L0_ffn_eb3': 8.0}
    for name, (base, spread) in spreads.items():
        noise = np.random.default_rng([zlib.crc32(name.encode()), seed]).standard_normal(out[name].shape)
        drawn = base * np.exp(spread * noise) if base else spread * noise
        out[name] = jnp.asarray(drawn.astype(out[name].dtype))
    for name, factor in factors.items():
        out[name] = (out[name] * factor).astype(out[name].dtype)
    return out
```

```python
from contextlib import ExitStack

import concourse.bass as bass
from concourse import mybir

P = 128
ALU = mybir.AluOpType
ACT = mybir.ActivationFunctionType
AX_X = mybir.AxisListType.X
F32 = mybir.dt.float32
BF16 = mybir.dt.bfloat16
I32 = mybir.dt.int32
U32 = mybir.dt.uint32

MASKED = -1.0e30
TAKEN = -3.0e30


def adaln_moe_ffn(nc, x, cond, W0, b0, W1, b1, W2, b2, mix_w, mix_b,
                  router_w, router_b, router_bias,
                  ew1, eb1, ew2, eb2, ew3, eb3,
                  sw1, sb1, sw2, sb2, sw3, sb3, out):
    BS, IN_C, DIM = x.shape
    EMB, HID = W0.shape
    KMIX = W2.shape[1]
    E, _, INTER = ew1.shape
    SHARED = sw1.shape[1]
    TOKENS = BS * IN_C
    TOPK = 2
    NGROUPS, GSIZE = 4, E // 4
    NT = TOKENS // P
    C = DIM // P
    BPT = P // IN_C
    KC = KMIX * IN_C // P
    KPC = KMIX // KC
    GT = 4
    NG = NT // GT
    EARLY = NG // 2
    GN = GT * P
    IB = SHARED // P
    ASSIGN = TOKENS * TOPK
    TILES = (ASSIGN + E * (P - 1)) // P
    TW = TILES + 1
    RING = 4

    x_rows = x.rearrange("b c d -> (b c) d")
    out_rows = out.rearrange("b c d -> (b c) d")
    xt_dram = nc.dram_tensor("xt_rows", [TOKENS, DIM], F32, kind="Internal").ap()
    y_dram = nc.dram_tensor("expert_rows", [ASSIGN, DIM], F32, kind="Internal").ap()

    ctx = ExitStack()
    with ctx:
        def sb(name, shape, dt=F32):
            return ctx.enter_context(nc.sbuf_tensor(name, shape, dt))

        def sem(name):
            return ctx.enter_context(nc.semaphore(name))

        w12 = sb("w12", [P, 2, E * C, INTER])
        w3 = sb("w3", [P, E, DIM])
        ebias = sb("ebias", [P, E, 2, INTER])
        sw12 = sb("sw12", [P, 2, C, SHARED])
        sw3_sb = sb("sw3_sb", [P, IB, DIM])
        x_early = sb("x_early", [P, EARLY * GT, DIM])
        late_region = sb("late_region", [P, 16384 // 4])
        xT = sb("xT", [P, NG, C, GN])
        r1 = sb("r1", [P, 8192 // 4])
        xt_sb = sb("xt_sb", [P, 8192 // 4])

        x_late = late_region[:, :].rearrange("p (t d) -> p t d", d=DIM)
        onehot_slot = late_region[:, 0:2048].bitcast(BF16).rearrange("p (j s) -> p j s", s=P)
        temps = late_region[:, 2048:4096].rearrange("p (n f) -> p n f", f=NT * E)
        S, mk, cc, oh1, oh2, t5 = (temps[:, n, :] for n in range(6))
        last_temps = late_region[:, 2048 + 6 * NT * E:4096]
        gate17 = last_temps[:, 0:NT * (E + 1)].rearrange("p (t e) -> p t e", e=E + 1)
        chosen = last_temps[:, 272:272 + 128].bitcast(BF16)
        pos = last_temps[:, 400:432].rearrange("p (k t) -> p k t", k=TOPK)
        pos_i = last_temps[:, 432:464].bitcast(I32).rearrange("p (k t) -> p k t", k=TOPK)
        ptile = last_temps[:, 464:496].rearrange("p (k t) -> p k t", k=TOPK)
        xg = late_region[:, 0:2048].rearrange("p (r d) -> p r d", d=DIM)
        y_sb = late_region[:, 2048:4096].rearrange("p (r d) -> p r d", d=DIM)

        mixT = r1[:, :].rearrange("p (t m) -> p t m", m=P)
        tile_code = r1[:, 0:1536].bitcast(BF16).rearrange("p (j v t) -> p j v t", v=2, t=TW)
        xgT = r1[:, 0:1024].rearrange("p (r c n) -> p r c n", r=2, c=C)
        h_sb = r1[:, 1024:1536].rearrange("p (r w n) -> p r w n", r=2, w=2)
        s_sb = r1[:, 1536:1792].rearrange("p (r n) -> p r n", r=2)
        g_sb = r1[:, 1792:2048].rearrange("p (r n) -> p r n", r=2)

        xt_ring = xt_sb[:, :].rearrange("p (r d) -> p r d", d=DIM)
        gs_sb = xt_sb[:, 0:1024].rearrange("p (i n) -> p i n", i=IB)
        eb3x = xt_sb[0:E + 1, 1024:1536]
        gT_sb = xt_sb[:, 1536:1792].rearrange("p (r n) -> p r n", r=2)

        slot_iota = xt_sb[:, 1792:1792 + P]

        cpool = xT[:, 0, :, :].rearrange("p c n -> p (c n)")
        cpos = [0]

        def early(rows, cols):
            a = cpool[0:rows, cpos[0]:cpos[0] + cols]
            cpos[0] += cols
            return a

        cond_sb, W0_sb, W1_sb, W2_sb = early(BS, EMB), early(P, HID), early(P, HID), early(P, KMIX)
        b0_sb, b1_sb, b2_sb = early(P, 1), early(P, 1), early(BS, KMIX)
        wk_sb = early(IN_C, KMIX * IN_C)
        condT, h1T, h2T = early(P, BS), early(P, BS), early(P, BS)
        att, att_e = early(BS, KMIX), early(BS, KMIX)
        att_max, att_sum, att_rec = early(BS, 1), early(BS, 1), early(BS, 1)
        att_rep = early(BS, KMIX * IN_C)
        mix_wT = early(P, KC * (IN_C + 1)).rearrange("p (k o) -> p k o", k=KC)
        diag32 = early(P, IN_C)
        attK = xT[:, 2:4, :, :].rearrange("p g c n -> p (g c n)").rearrange("p (k b i) -> p k b i", k=KC, b=BS)
        gateT = xT[0:E + 1, 0, :, :].rearrange("p c n -> p (c n)")

        w12_flat = w12[:, :, :, :].rearrange("p w e n -> p (w e n)")
        rows_k = w12_flat[:, 0:2 * TOPK * GT * DIM].rearrange("p (b k t d) -> p b k t d", b=2, k=TOPK, t=GT)
        x_again = w12_flat[:, 8192:8192 + 8 * DIM].rearrange("p (t d) -> p t d", d=DIM)

        ident = sb("ident", [P, P])
        before = sb("before", [P, P], BF16)
        ones_bf = sb("ones_bf", [P, P], BF16)
        rw_sb = sb("rw_sb", [P, C, E])
        rb_sb = sb("rb_sb", [P, E])
        rbias_sb = sb("rbias_sb", [P, E])
        sb12_sb = sb("sb12_sb", [P, 2, IB])
        mix_bias = sb("mix_bias", [P, NT])
        rev_e = sb("rev_e", [P, E])
        tile_iota = sb("tile_iota", [P, TW])
        part_iota = sb("part_iota", [P, 1])
        hi_code = sb("hi_code", [P, TOPK * NT])
        lower = sb("lower", [P, NGROUPS, NGROUPS])
        restart = sb("restart", [P, NT])
        steps128 = sb("steps128", [P, NT])
        tops = sb("tops", [P, TOPK, NT])
        small = sb("small", [P, 4, NT])
        count = sb("count", [P, 4, E])
        pslot = sb("pslot", [P, TOPK, NT])
        tile_expert = sb("tile_expert", [P, TW], I32)
        code_f = sb("code_f", [P, TW])
        to_row = sb("to_row", [P, TW], I32)
        from_row = sb("from_row", [P, TW], I32)
        to_slot = sb("to_slot", [P, RING], I32)
        from_slot = sb("from_slot", [P, RING], I32)

        psum = ctx.enter_context(nc.psum_tensor("psum", [P, 8, 512], F32))

        cond_loaded = sem("cond_loaded")
        x_loaded = [sem(f"x_loaded{g}") for g in range(NG)]
        router_loaded = sem("router_loaded")
        shared_loaded = sem("shared_loaded")
        experts_loaded = sem("experts_loaded")
        eb3_loaded = sem("eb3_loaded")
        consts_ready = sem("consts_ready")
        slots_ready = sem("slots_ready")
        pool_chain = sem("pool_chain")
        dve_chain = sem("dve_chain")
        act_chain = sem("act_chain")
        pe_cond = sem("pe_cond")
        dve_cond = sem("dve_cond")
        act_cond = sem("act_cond")
        mix_done = sem("mix_done")
        mix_copied = sem("mix_copied")
        mix_copied_act = sem("mix_copied_act")
        xt_done = sem("xt_done")
        xt_ready = sem("xt_ready")
        xt_stored = [sem(f"xt_stored{r}") for r in range(RING)]
        xtT_done = sem("xtT_done")
        xT_ready = sem("xT_ready")
        logits_done = sem("logits_done")
        shifted_ready = sem("shifted_ready")
        exp_ready = sem("exp_ready")
        gates_ready = sem("gates_ready")
        gateT_done = sem("gateT_done")
        gateT_ready = sem("gateT_ready")
        chosen_ready = sem("chosen_ready")
        ranks_done = sem("ranks_done")
        codes_ready = sem("codes_ready")
        dispatch_done = sem("dispatch_done")
        tables_ready = sem("tables_ready")
        up_done = sem("up_done")
        up_silu = sem("up_silu")
        up_ready = sem("up_ready")
        down_done = sem("down_done")
        z_ready = sem("z_ready")
        idx_copied = sem("idx_copied")
        pool_held = sem("pool_held")
        xg_loaded = [sem(f"xg_loaded{r}") for r in range(RING)]
        xgT_done = sem("xgT_done")
        xgT_ready = sem("xgT_ready")
        h_done = sem("h_done")
        h_ready = sem("h_ready")
        s_ready = sem("s_ready")
        g_ready = sem("g_ready")
        gT_done = sem("gT_done")
        gT_ready = sem("gT_ready")
        y_done = sem("y_done")
        y_ready = sem("y_ready")
        scattered = [sem(f"scattered{r}") for r in range(RING)]
        all_scattered = sem("all_scattered")
        x_again_loaded = sem("x_again_loaded")
        rows_loaded = [sem(f"rows_loaded{g}") for g in range(NG)]
        out_ready = sem("out_ready")
        out_stored = sem("out_stored")

        EXPERT_LOADS = 2 + 1 + 2

        block = ctx.enter_context(nc.Block())

        def x_tile(t):
            return x_early[:, t, :] if t < EARLY * GT else x_late[:, t - EARLY * GT, :]

        def xT_tile(t, c):
            return xT[:, t // GT, c, (t % GT) * P:(t % GT + 1) * P]

        def store_group(sp, g):
            for t in range(g * GT, (g + 1) * GT):
                sp.wait_ge(*((out_ready, t + 1) if t < EARLY * GT else (z_ready, t + 1)))
                src = x_early[:, t, :] if t < EARLY * GT else x_again[:, t - EARLY * GT, :]
                sp.dma_start(out_rows[t * P:(t + 1) * P, :], src).then_inc(out_stored, 16)

        @block.sync
        def _(sp):
            with nc.allow_non_contiguous_dma(reason="a few small vectors"):
                small_loads = [
                    (cond_sb, cond), (W0_sb, W0), (b0_sb, b0.rearrange("(p o) -> p o", o=1)),
                    (W1_sb, W1), (b1_sb, b1.rearrange("(p o) -> p o", o=1)), (W2_sb, W2),
                    (b2_sb, b2.rearrange("(o k) -> o k", o=1).to_broadcast([BS, KMIX])),
                    (wk_sb.rearrange("o (k i) -> o k i", k=KMIX), mix_w.rearrange("k o i u -> o k (i u)")),
                    (mix_wT[:, :, IN_C], mix_b.rearrange("(c k) i -> (k i) c", c=KC)),
                ]
                for dst, src in small_loads:
                    sp.dma_start(dst, src).then_inc(cond_loaded, 16)
                for g in range(NG):
                    dst = x_early[:, g * GT:(g + 1) * GT, :] if g < EARLY else \
                        x_late[:, (g - EARLY) * GT:(g - EARLY + 1) * GT, :]
                    sp.dma_start(dst, x_rows[g * GN:(g + 1) * GN, :].rearrange("(t p) d -> p t d", p=P)
                                 ).then_inc(x_loaded[g], 16)
                sp.dma_start(rw_sb[:, :, :], router_w.rearrange("(c p) e -> p c e", p=P)).then_inc(router_loaded, 16)
                sp.dma_start(rb_sb[:, :], router_b.rearrange("(o e) -> o e", o=1).to_broadcast([P, E])
                             ).then_inc(router_loaded, 16)
                sp.dma_start(rbias_sb[:, :], router_bias.rearrange("(o e) -> o e", o=1).to_broadcast([P, E])
                             ).then_inc(router_loaded, 16)
                sp.dma_start(sw12[:, 0], sw1.rearrange("(c p) n -> p c n", p=P)).then_inc(shared_loaded, 16)
                sp.dma_start(sw12[:, 1], sw2.rearrange("(c p) n -> p c n", p=P)).then_inc(shared_loaded, 16)
                sp.dma_start(sb12_sb[:, 0], sb1.rearrange("(i p) -> p i", p=P)).then_inc(shared_loaded, 16)
                sp.dma_start(sb12_sb[:, 1], sb2.rearrange("(i p) -> p i", p=P)).then_inc(shared_loaded, 16)
                sp.dma_start(sw3_sb[:, :, :], sw3.rearrange("(i p) n -> p i n", p=P)).then_inc(shared_loaded, 16)
            for t in range(NT):
                sp.wait_ge(xt_ready, t + 1)
                sp.dma_start(xt_dram[t * P:(t + 1) * P, :], xt_ring[:, t % RING, :]
                             ).then_inc(xt_stored[t % RING], 16)
            for r in range(RING):
                sp.wait_ge(xt_stored[r], 16 * (NT // RING))
            sp.wait_ge(xtT_done, NT)
            sp.dma_start(eb3x[0:E, :], eb3).then_inc(eb3_loaded, 16)
            sp.dma_start(eb3x[E:E + 1, :], sb3.rearrange("(o n) -> o n", o=1)).then_inc(eb3_loaded, 16)
            sp.wait_ge(y_done, TILES)
            sp.dma_start(x_again[:, :, :], x_rows[EARLY * GN:NG * GN, :].rearrange("(t p) d -> p t d", p=P)
                         ).then_inc(x_again_loaded, 16)
            for r in range(RING):
                sp.wait_ge(scattered[r], 16 * ((TILES - 1 - r) // RING + 1))
            for g in range(NG):
                if g >= 2:
                    sp.wait_ge(out_ready, (g - 1) * GT)
                for k in range(TOPK):
                    src = y_dram[k * TOKENS + g * GN:k * TOKENS + (g + 1) * GN, :]
                    sp.dma_start(rows_k[:, g % 2, k], src.rearrange("(t p) d -> p t d", p=P)
                                 ).then_inc(rows_loaded[g], 16)
                if g >= 1:
                    store_group(sp, g - 1)
            store_group(sp, NG - 1)
            sp.wait_ge(out_stored, 16 * NT)

        @block.gpsimd
        def _(pool):
            n = [0]

            def link(ins):
                n[0] += 1
                ins.then_inc(pool_chain, 1)
                pool.wait_ge(pool_chain, n[0])

            link(nc.gpsimd.memset(ident[:, :], 0.0))
            link(nc.gpsimd.affine_select(out=ident[:, :], in_=ident[:, :], compare_op=ALU.not_equal, fill=1.0,
                                         base=0, pattern=[[-1, P]], channel_multiplier=1))
            link(nc.gpsimd.memset(diag32[:, :], 0.0))
            for b in range(BPT):
                link(nc.gpsimd.affine_select(out=diag32[:, :], in_=diag32[:, :], compare_op=ALU.not_equal,
                                             fill=1.0, base=-IN_C * b, pattern=[[-1, IN_C]],
                                             channel_multiplier=1))
            link(nc.gpsimd.memset(r1[:, :], 0.0))
            link(nc.gpsimd.memset(ones_bf[:, :], 1.0))
            link(nc.gpsimd.affine_select(out=before[:, :], in_=ones_bf[:, :], compare_op=ALU.is_gt, fill=0.0,
                                         base=0, pattern=[[1, P]], channel_multiplier=-1))
            for dst, pattern, base, mult in (
                    (rev_e[:, :], [[-1, E]], E, 0),
                    (tile_iota[:, :], [[1, TW]], 0, 0), (part_iota[:, :], [[1, 1]], 0, 1),
                    (hi_code[:, :], [[-1, TOPK * NT]], TOPK * NT, 0),
                    (restart[:, :], [[1, NT]], 0, 0), (steps128[:, :], [[P, NT]], 0, 0),
                    (lower[:, :, :], [[1, NGROUPS], [-1, NGROUPS]], 0, 0)):
                link(nc.gpsimd.iota(dst, pattern=pattern, base=base, channel_multiplier=mult,
                                    allow_small_or_imprecise_dtypes=True))
            link(nc.gpsimd.tensor_scalar(restart[:, :], restart[:, :], 1.0, None, ALU.min))
            link(nc.gpsimd.tensor_scalar(lower[:, :, :], lower[:, :, :], 0.0, None, ALU.is_gt))
            nc.gpsimd.memset(to_slot[:, :], 0).then_inc(consts_ready, 1)

            pool.wait_ge(xtT_done, NT)
            for r in range(RING):
                pool.wait_ge(xt_stored[r], 16 * (NT // RING))
            nc.gpsimd.iota(slot_iota, pattern=[[1, P]], base=0, channel_multiplier=0,
                           allow_small_or_imprecise_dtypes=True).then_inc(slots_ready, 1)
            pool.wait_ge(tables_ready, 1)

            def hold(semaphore, value):
                pool.wait_ge(semaphore, value)
                pool.sem_inc(pool_held, 1)

            def gather(i, slot, copied):
                nc.gpsimd.tensor_copy(from_slot[:, slot:slot + 1], from_row[:, bass.ds(i, 1)]
                                      ).then_inc(idx_copied, 1)
                hold(idx_copied, copied)
                nc.gpsimd.indirect_dma_start(
                    out=xg[:, slot, :], out_offset=None, in_=xt_dram[:, :],
                    in_offset=bass.IndirectOffsetOnAxis(ap=from_slot[:, slot:slot + 1].bitcast(U32), axis=0),
                ).then_inc(xg_loaded[slot], 16)

            def scatter(i, slot, copied):
                nc.gpsimd.tensor_copy(to_slot[:, slot:slot + 1], to_row[:, bass.ds(i, 1)]
                                      ).then_inc(idx_copied, 1)
                hold(idx_copied, copied)
                nc.gpsimd.indirect_dma_start(
                    out=y_dram[:, :],
                    out_offset=bass.IndirectOffsetOnAxis(ap=to_slot[:, slot:slot + 1].bitcast(U32), axis=0),
                    in_=y_sb[:, slot, :], in_offset=None, bounds_check=ASSIGN - 1, oob_is_err=False,
                ).then_inc(scattered[slot], 16)

            def pool_step(i, j, u):
                hold(xgT_done, i + 1)
                gather(i + RING, u, 2 * i + RING + 1)
                hold(y_ready, i + 1)
                scatter(i, u, 2 * i + RING + 2)

            for i in range(RING):
                gather(i, i, i + 1)
            looped = (TILES - RING) // RING
            with pool.Fori(0, looped) as j:
                for u in range(RING):
                    pool_step(j * RING + u, j, u)
            for i in range(looped * RING, TILES - RING):
                pool_step(i, i // RING, i % RING)
            for i in range(TILES - RING, TILES):
                hold(y_ready, i + 1)
                scatter(i, i % RING, TILES + i + 1)

        @block.tensor
        def _(pe):
            def mm(dst, lhsT, rhs, start=True, stop=True):
                return nc.tensor.matmul(dst, lhsT, rhs, start=start, stop=stop)

            pe.wait_ge(cond_loaded, 16 * 9)
            pe.wait_ge(consts_ready, 1)
            nc.tensor.transpose(psum[:, 0, 0:BS], cond_sb, ident[0:BS, 0:BS])
            for k in range(KC):
                last = nc.tensor.transpose(psum[:, 1, k * IN_C:(k + 1) * IN_C], wk_sb[:, k * P:(k + 1) * P],
                                           ident[0:IN_C, 0:IN_C])
            last.then_inc(pe_cond, 1)
            pe.wait_ge(dve_cond, 1)
            mm(psum[:, 2, 0:BS], W0_sb, condT).then_inc(pe_cond, 1)
            pe.wait_ge(act_cond, 1)
            mm(psum[:, 3, 0:BS], W1_sb, h1T).then_inc(pe_cond, 1)
            pe.wait_ge(act_cond, 2)
            mm(psum[0:BS, 4, 0:KMIX], h2T, W2_sb).then_inc(pe_cond, 1)
            pe.wait_ge(dve_cond, 3)
            for k in range(KC):
                last = nc.tensor.transpose(psum[:, 5 + k, 0:BS], att_rep[:, k * P:(k + 1) * P],
                                           ident[0:BS, 0:BS])
            last.then_inc(pe_cond, 1)
            pe.wait_ge(dve_cond, 5)
            for t in range(NT):
                for k in range(KC):
                    last = mm(psum[:, t // 8, (t % 8) * 33:(t % 8) * 33 + 33],
                              attK[:, k, t * BPT:(t + 1) * BPT, :].rearrange("p b i -> p (b i)"),
                              mix_wT[:, k, :], start=(k == 0), stop=(k == KC - 1))
            last.then_inc(mix_done, 1)

            pe.wait_ge(mix_copied, 1)
            pe.wait_ge(mix_copied_act, 1)
            for s in range(NT + 2):
                if s < NT:
                    if s % GT == 0:
                        pe.wait_ge(x_loaded[s // GT], 16)
                    if s >= 2:
                        pe.wait_ge(xt_ready, s - 1)
                    mm(psum[:, s % 2, :], mixT[:, s, :], x_tile(s)).then_inc(xt_done, 1)
                if 1 <= s <= NT:
                    t = s - 1
                    pe.wait_ge(xt_ready, t + 1)
                    if t >= 2:
                        pe.wait_ge(xT_ready, t - 1)
                    for c in range(C):
                        last = nc.tensor.transpose(psum[:, 2 + t % 2, c * P:(c + 1) * P],
                                                   xt_ring[:, t % RING, c * P:(c + 1) * P], ident[:, :])
                    last.then_inc(xtT_done, 1)
                if s >= 2:
                    t = s - 2
                    if t == 0:
                        pe.wait_ge(router_loaded, 48)
                    pe.wait_ge(xT_ready, t + 1)
                    for c in range(C):
                        last = mm(psum[:, 4, t * E:(t + 1) * E], xT_tile(t, c), rw_sb[:, c, :],
                                  start=(c == 0), stop=(c == C - 1))
            last.then_inc(logits_done, 1)

            def shared_up(g):
                for i in range(IB):
                    n = g * IB + i
                    if n >= 2:
                        pe.wait_ge(up_ready, n - 1)
                    for w in range(2):
                        for c in range(C):
                            last = mm(psum[:, 2 * i + w, :], sw12[:, w, c, i * P:(i + 1) * P], xT[:, g, c, :],
                                      start=(c == 0), stop=(c == C - 1))
                    last.then_inc(up_done, 1)

            def shared_down(g):
                pe.wait_ge(up_ready, IB * (g + 1))
                for t in range(g * GT, (g + 1) * GT):
                    if t >= GT:
                        pe.wait_ge(z_ready, t - GT + 1)
                    bank = psum[:, 4 + t % GT, :]
                    for i in range(IB):
                        mm(bank, gs_sb[:, i, (t % GT) * P:(t % GT + 1) * P], sw3_sb[:, i, :],
                           start=(i == 0), stop=False)
                    mm(bank, gateT[:, t * P:(t + 1) * P], eb3x, start=False, stop=True).then_inc(down_done, 1)

            pe.wait_ge(shared_loaded, 80)
            shared_up(0)
            pe.wait_ge(gates_ready, 1)
            for t in range(NT):
                last = nc.tensor.transpose(psum[0:E + 1, 4 + t // GT, (t % GT) * P:(t % GT + 1) * P],
                                           gate17[:, t, :], ident[:, :])
            last.then_inc(gateT_done, 1)
            pe.wait_ge(chosen_ready, 1)
            pe.wait_ge(up_ready, 2)
            mm(psum[:, 0, 0:NT * E], before[:, :], chosen)
            mm(psum[:, 1, 0:NT * E], ones_bf[:, :], chosen).then_inc(ranks_done, 1)
            pe.wait_ge(gateT_ready, 1)
            pe.wait_ge(eb3_loaded, 32)
            shared_down(0)
            pe.wait_ge(codes_ready, 1)
            shared_up(1)
            pe.wait_ge(up_ready, 2 * IB)
            for j in range(TOPK * NT):
                last = mm(psum[:, 0, 0:2 * TW], onehot_slot[:, j, :],
                          tile_code[:, j, :, :].rearrange("p v t -> p (v t)"),
                          start=(j == 0), stop=(j == TOPK * NT - 1))
            last.then_inc(dispatch_done, 1)
            shared_down(1)

            pe.wait_ge(experts_loaded, 16 * EXPERT_LOADS)
            pe.wait_ge(z_ready, EARLY * GT)
            pe.wait_ge(tables_ready, 1)

            def rows_transposed(b, slot, loaded):
                pe.wait_ge(xg_loaded[slot], loaded)
                for c in range(C):
                    last = nc.tensor.transpose(psum[:, b, c * P:(c + 1) * P], xg[:, slot, c * P:(c + 1) * P],
                                               ident[:, :])
                last.then_inc(xgT_done, 1)

            def up(b, e, half):
                for c in range(half * C // 2, (half + 1) * C // 2):
                    last = mm(psum[:, 2 + b, 0:2 * INTER].rearrange("p (w n) -> p w n", w=2), xgT[:, b, c, :],
                              w12[:, :, bass.ds(e * C + c, 1), :].rearrange("p w u n -> p w (u n)"),
                              start=(c == 0), stop=(c == C - 1))
                return last

            def down(b, e):
                mm(psum[:, 6 + b, :], gT_sb[:, b, :],
                   w3[:, bass.ds(e, 1), :].rearrange("p u n -> p (u n)")).then_inc(y_done, 1)

            def expert_of(i):
                return pe.value_load(tile_expert[0:1, bass.ds(i, 1)], min_val=0, max_val=E - 1)

            def pe_step(i, b, slot_next, loaded_next, first=False, last=False):
                e = expert_of(i)
                pe.wait_ge(xgT_ready, i + 1)
                up(b, e, 0)
                if not first:
                    pe.wait_ge(g_ready, i)
                    nc.tensor.transpose(psum[:, 4 + (1 - b), 0:P], g_sb[:, 1 - b, :], ident[:, :]
                                        ).then_inc(gT_done, 1)
                up(b, e, 1).then_inc(h_done, 1)
                if not last:
                    rows_transposed(1 - b, slot_next, loaded_next)
                if not first:
                    e_before = expert_of(i - 1)
                    pe.wait_ge(gT_ready, i)
                    if not isinstance(i, int) or i >= 3:
                        pe.wait_ge(y_ready, i - 2)
                    down(1 - b, e_before)

            rows_transposed(0, 0, 16)
            pe_step(0, 0, 1, 16, first=True)
            for i in range(1, 3):
                pe_step(i, i % 2, (i + 1) % RING, 16 * ((i + 1) // RING + 1))
            PEELED = 3
            looped = (TILES - 1 - PEELED) // RING
            with pe.Fori(0, looped) as j:
                for u in range(RING):
                    k = PEELED + u
                    pe_step(j * RING + k, k % 2, (k + 1) % RING, j * 16 + 16 * ((k + 1) // RING + 1))
            for i in range(PEELED + looped * RING, TILES):
                pe_step(i, i % 2, (i + 1) % RING, 16 * ((i + 1) // RING + 1), last=(i == TILES - 1))
            b = (TILES - 1) % 2
            pe.wait_ge(g_ready, TILES)
            nc.tensor.transpose(psum[:, 4 + b, 0:P], g_sb[:, b, :], ident[:, :]).then_inc(gT_done, 1)
            e = expert_of(TILES - 1)
            pe.wait_ge(gT_ready, TILES)
            pe.wait_ge(y_ready, TILES - 2)
            down(b, e)

            shared_up(2)
            pe.wait_ge(y_ready, TILES)
            shared_down(2)
            shared_up(3)
            shared_down(3)

        @block.scalar
        def _(act):
            for w, src in ((0, ew1), (1, ew2)):
                act.dma_start(w12[:, w], src.rearrange("e (c p) n -> p (e c) n", p=P)).then_inc(experts_loaded, 16)
            act.dma_start(w3[:, :, :], ew3.rearrange("e p n -> p e n")).then_inc(experts_loaded, 16)
            for w, src in ((0, eb1), (1, eb2)):
                act.dma_start(ebias[:, :, w, :],
                              src.rearrange("(o e) n -> o e n", o=1).to_broadcast([P, E, INTER])
                              ).then_inc(experts_loaded, 16)
            act.wait_ge(pe_cond, 2)
            act.wait_ge(cond_loaded, 16 * 9)
            nc.scalar.activation(h1T, psum[:, 2, 0:BS], ACT.Gelu, bias=b0_sb).then_inc(act_cond, 1)
            act.wait_ge(pe_cond, 3)
            nc.scalar.activation(h2T, psum[:, 3, 0:BS], ACT.Gelu, bias=b1_sb).then_inc(act_cond, 1)
            act.wait_ge(dve_cond, 2)
            nc.scalar.activation(att_e, att, ACT.Exp, accum_out=att_sum).then_inc(act_cond, 1)
            act.wait_ge(mix_done, 1)
            act.wait_ge(consts_ready, 1)
            blocks = psum[:, 1, 0:8 * 33].rearrange("p (t o) -> p t o", o=33)
            nc.scalar.activation(mix_bias[:, 8:16], blocks[:, :, IN_C], ACT.Copy)
            for b in range(BPT):
                rows = slice(b * IN_C, (b + 1) * IN_C)
                last = nc.scalar.activation(mixT[rows, 8:16, b * IN_C:(b + 1) * IN_C],
                                            blocks[rows, :, 0:IN_C], ACT.Copy)
            last.then_inc(mix_copied_act, 1)
            act.wait_ge(mix_copied, 1)
            act.wait_ge(mix_copied_act, 1)
            for t in range(NT):
                act.wait_ge(xt_done, t + 1)
                if t >= RING:
                    act.wait_ge(xt_stored[t % RING], 16 * (t // RING))
                    act.wait_ge(xtT_done, t - RING + 1)
                nc.scalar.activation(xt_ring[:, t % RING, :], psum[:, t % 2, :], ACT.Identity,
                                     bias=mix_bias[:, t:t + 1]).then_inc(xt_ready, 1)
            act.wait_ge(shifted_ready, 1)
            nc.scalar.activation(mk, S, ACT.Exp).then_inc(exp_ready, 1)

            def shared_silu(g):
                for i in range(IB):
                    act.wait_ge(up_done, g * IB + i + 1)
                    if g >= 1:
                        act.wait_ge(down_done, g * GT)
                    nc.scalar.activation(gs_sb[:, i, :], psum[:, 2 * i, :], ACT.Silu, bias=sb12_sb[:, 0, i:i + 1]
                                         ).then_inc(up_silu, 1)

            act.wait_ge(shared_loaded, 80)
            act.wait_ge(xtT_done, NT)
            for r in range(RING):
                act.wait_ge(xt_stored[r], 16 * (NT // RING))
            shared_silu(0)
            act.wait_ge(gateT_done, 1)
            for q in range(NG):
                last = nc.scalar.activation(gateT[:, q * GN:(q + 1) * GN], psum[0:E + 1, 4 + q, :], ACT.Copy)
            last.then_inc(gateT_ready, 1)
            shared_silu(1)

            def hidden_transposed(b, done):
                act.wait_ge(gT_done, done)
                nc.scalar.activation(gT_sb[:, b, :], psum[:, 4 + b, 0:P], ACT.Copy).then_inc(gT_ready, 1)

            def silu(b, done):
                act.wait_ge(h_ready, done)
                nc.scalar.activation(s_sb[:, b, :], h_sb[:, b, 0, :], ACT.Silu).then_inc(s_ready, 1)

            def result(b, slot, done, freed):
                act.wait_ge(y_done, done)
                if freed is not None:
                    act.wait_ge(scattered[slot], freed)
                nc.scalar.activation(y_sb[:, slot, :], psum[:, 6 + b, :], ACT.Copy).then_inc(y_ready, 1)

            silu(0, 1)
            for i in range(1, RING + 1):
                hidden_transposed((i - 1) % 2, i)
                silu(i % 2, i + 1)
                result((i - 1) % 2, i - 1, i, None)
            PEELED = RING + 1
            looped = (TILES - PEELED) // RING
            with act.Fori(0, looped) as j:
                for u in range(RING):
                    k = PEELED + u
                    i = j * RING + k
                    hidden_transposed((k - 1) % 2, i)
                    silu(k % 2, i + 1)
                    result((k - 1) % 2, (k - 1) % RING, i, j * 16 + 16 * ((k - 1) // RING))
            for i in range(PEELED + looped * RING, TILES):
                hidden_transposed((i - 1) % 2, i)
                silu(i % 2, i + 1)
                result((i - 1) % 2, (i - 1) % RING, i, 16 * ((i - 1) // RING))
            hidden_transposed((TILES - 1) % 2, TILES)
            result((TILES - 1) % 2, (TILES - 1) % RING, TILES, 16 * ((TILES - 1) // RING))
            shared_silu(2)
            shared_silu(3)

        @block.vector
        def _(dve):
            n = [0]

            def link(ins):
                n[0] += 1
                ins.then_inc(dve_chain, 1)
                dve.wait_ge(dve_chain, n[0])

            def tt(dst, a, b, op):
                return nc.vector.tensor_tensor(dst, a, b, op)

            V = nc.vector
            dve.wait_ge(pe_cond, 1)
            V.tensor_copy(condT, psum[:, 0, 0:BS])
            V.tensor_copy(mix_wT[:, :, 0:IN_C], psum[:, 1, 0:KC * IN_C].rearrange("p (k o) -> p k o", k=KC)
                          ).then_inc(dve_cond, 1)
            dve.wait_ge(pe_cond, 4)
            dve.wait_ge(cond_loaded, 16 * 9)
            link(tt(att, psum[0:BS, 4, 0:KMIX], b2_sb, ALU.add))
            link(V.tensor_reduce(att_max, att, AX_X, ALU.max))
            V.tensor_scalar(att, att, att_max, None, ALU.subtract).then_inc(dve_cond, 1)
            dve.wait_ge(act_cond, 3)
            link(V.reciprocal(att_rec, att_sum))
            V.tensor_scalar(att_rep.rearrange("b (k i) -> b k i", k=KMIX),
                            att_e.unsqueeze(2).to_broadcast([BS, KMIX, IN_C]), att_rec, None, ALU.mult
                            ).then_inc(dve_cond, 1)
            dve.wait_ge(pe_cond, 5)
            dve.wait_ge(consts_ready, 1)
            for k in range(KC):
                tt(attK[:, k], psum[:, 5 + k, 0:BS].unsqueeze(2).to_broadcast([P, BS, IN_C]),
                   diag32.unsqueeze(1).to_broadcast([P, BS, IN_C]), ALU.mult).then_inc(dve_cond, 1)
            dve.wait_ge(mix_done, 1)
            blocks = psum[:, 0, 0:8 * 33].rearrange("p (t o) -> p t o", o=33)
            V.tensor_copy(mix_bias[:, 0:8], blocks[:, :, IN_C])
            for b in range(BPT):
                rows = slice(b * IN_C, (b + 1) * IN_C)
                last = V.tensor_copy(mixT[rows, 0:8, b * IN_C:(b + 1) * IN_C], blocks[rows, :, 0:IN_C])
            last.then_inc(mix_copied, 1)
            for t in range(NT):
                dve.wait_ge(xtT_done, t + 1)
                V.tensor_copy(xT[:, t // GT, :, (t % GT) * P:(t % GT + 1) * P],
                              psum[:, 2 + t % 2, :].rearrange("p (c n) -> p c n", c=C)).then_inc(xT_ready, 1)

            def te(a):
                return a.rearrange("p (t e) -> p t e", e=E)

            def over_e(a):
                return a.unsqueeze(2).to_broadcast([P, NT, E])

            def over_t(a):
                return a.unsqueeze(1).to_broadcast([P, NT, E])

            dve.wait_ge(logits_done, 1)
            dve.wait_ge(router_loaded, 48)
            link(tt(te(S), te(psum[:, 4, 0:NT * E]), over_t(rb_sb[:, :]), ALU.add))
            link(V.tensor_reduce(small[:, 0, :], te(S), AX_X, ALU.max))
            tt(te(S), te(S), over_e(small[:, 0, :]), ALU.subtract).then_inc(shifted_ready, 1)
            dve.wait_ge(exp_ready, 1)
            link(V.tensor_reduce(small[:, 0, :], te(mk), AX_X, ALU.add))
            link(V.reciprocal(small[:, 1, :], small[:, 0, :]))
            link(tt(te(S), te(mk), over_e(small[:, 1, :]), ALU.mult))
            link(tt(te(S), te(S), over_t(rbias_sb[:, :]), ALU.add))

            gmax = cc[:, 0:NT * NGROUPS]
            link(V.tensor_reduce(gmax, S.rearrange("p (n s) -> p n s", s=GSIZE), AX_X, ALU.max))
            gm = gmax.rearrange("p (t g) -> p t g", g=NGROUPS)
            other = gm.unsqueeze(2).to_broadcast([P, NT, NGROUPS, NGROUPS])
            own = gm.unsqueeze(3).to_broadcast([P, NT, NGROUPS, NGROUPS])

            def tgg(a):
                return a.rearrange("p (t g h) -> p t g h", g=NGROUPS, h=NGROUPS)

            tt(tgg(oh1), other, own, ALU.is_gt)
            link(tt(tgg(oh2), other, own, ALU.is_equal))
            link(tt(tgg(oh2), tgg(oh2), lower[:, :, :].unsqueeze(1).to_broadcast([P, NT, NGROUPS, NGROUPS]),
                    ALU.mult))
            link(tt(oh1, oh1, oh2, ALU.add))
            rank = t5[:, 0:NT * NGROUPS]
            keep = t5[:, NT * NGROUPS:2 * NT * NGROUPS]
            penalty = t5[:, 2 * NT * NGROUPS:3 * NT * NGROUPS]
            link(V.tensor_reduce(rank, oh1.rearrange("p (n h) -> p n h", h=NGROUPS), AX_X, ALU.add))
            V.tensor_scalar(keep, rank, 1.5, None, ALU.is_lt)
            link(V.tensor_scalar(penalty, rank, 1.5, MASKED, ALU.is_ge, ALU.mult))

            def per_group(a):
                return a.unsqueeze(2).to_broadcast([P, NT * NGROUPS, GSIZE])

            def ns(a):
                return a.rearrange("p (n s) -> p n s", s=GSIZE)

            link(tt(ns(mk), ns(S), per_group(keep), ALU.mult))
            link(tt(ns(mk), ns(mk), per_group(penalty), ALU.add))

            for k, oh in enumerate((oh1, oh2)):
                link(V.tensor_reduce(tops[:, k, :], te(mk), AX_X, ALU.max))
                link(tt(te(cc), te(mk), over_e(tops[:, k, :]), ALU.is_equal))
                link(tt(te(cc), te(cc), over_t(rev_e[:, :]), ALU.mult))
                link(V.tensor_reduce(small[:, 0, :], te(cc), AX_X, ALU.max))
                link(tt(te(oh), te(cc), over_e(small[:, 0, :]), ALU.is_equal))
                if k == 0:
                    link(V.scalar_tensor_tensor(out=mk, in0=oh, scalar=TAKEN, in1=mk, op0=ALU.mult, op1=ALU.add))
            tt(chosen, oh1, oh2, ALU.add).then_inc(chosen_ready, 1)
            V.memset(gate17[:, :, E:E + 1], 1.0)
            tt(te(S), te(oh1), over_e(tops[:, 0, :]), ALU.mult)
            link(tt(te(cc), te(oh2), over_e(tops[:, 1, :]), ALU.mult))
            tt(gate17[:, :, 0:E], te(S), te(cc), ALU.add).then_inc(gates_ready, 1)

            def shared_hidden(g):
                for i in range(IB):
                    dve.wait_ge(up_silu, g * IB + i + 1)
                    V.scalar_tensor_tensor(out=gs_sb[:, i, :], in0=psum[:, 2 * i + 1, :],
                                           scalar=sb12_sb[:, 1, i:i + 1], in1=gs_sb[:, i, :],
                                           op0=ALU.add, op1=ALU.mult).then_inc(up_ready, 1)

            dve.wait_ge(shared_loaded, 80)
            shared_hidden(0)

            dve.wait_ge(ranks_done, 1)
            tot, incl, excl = S, mk, cc
            cnt, ntile, end, base = (count[:, q, :] for q in range(4))

            def et(a):
                return a.rearrange("p (e t) -> p e t", t=NT)

            link(V.tensor_copy(et(tot), te(psum[:, 1, 0:NT * E]).rearrange("p t e -> p e t")))
            link(V.tensor_copy(et(t5), restart[:, :].unsqueeze(1).to_broadcast([P, E, NT])))
            link(V.tensor_tensor_scan(incl, t5, tot, 0.0, ALU.mult, ALU.add))
            tt(excl, incl, tot, ALU.subtract)
            link(V.tensor_copy(cnt, et(incl)[:, :, NT - 1]))
            link(tt(et(t5), cnt.unsqueeze(2).to_broadcast([P, E, NT]),
                    steps128[:, :].unsqueeze(1).to_broadcast([P, E, NT]), ALU.is_gt))
            link(V.tensor_reduce(ntile, et(t5), AX_X, ALU.add))
            link(V.memset(small[:, 2, :], 1.0))
            link(V.tensor_tensor_scan(end, small[:, 2, :], ntile, 0.0, ALU.mult, ALU.add))
            link(tt(base, end, ntile, ALU.subtract))
            link(V.tensor_scalar(base, base, float(P), None, ALU.mult))
            link(tt(te(S), te(psum[:, 0, 0:NT * E]), et(excl).rearrange("p e t -> p t e"), ALU.add))
            link(tt(te(S), te(S), over_t(base), ALU.add))
            for k, oh in enumerate((oh1, oh2)):
                link(tt(mk, oh, S, ALU.mult))
                link(V.tensor_reduce(pos[:, k, :], te(mk), AX_X, ALU.add))
            cmp = late_region[:, 2048:2048 + TW * E].rearrange("p (t e) -> p t e", e=E)
            link(tt(cmp, end.unsqueeze(1).to_broadcast([P, TW, E]),
                    tile_iota[:, :].unsqueeze(2).to_broadcast([P, TW, E]), ALU.is_le))
            link(V.tensor_reduce(code_f[:, :], cmp, AX_X, ALU.add))
            link(V.tensor_scalar(tile_expert[:, :], code_f[:, :], float(E - 1), None, ALU.min))
            link(V.tensor_copy(pos_i[:, :, :], pos[:, :, :]))
            link(V.tensor_scalar(pos_i[:, :, :], pos_i[:, :, :], 7, None, ALU.arith_shift_right))
            link(V.tensor_copy(ptile[:, :, :], pos_i[:, :, :]))
            link(V.scalar_tensor_tensor(out=pslot[:, :, :], in0=ptile[:, :, :], scalar=-float(P),
                                        in1=pos[:, :, :], op0=ALU.mult, op1=ALU.add))
            J = TOPK * NT
            pt = ptile[:, :, :].rearrange("p k t -> p (k t)")
            pp = pslot[:, :, :].rearrange("p k t -> p (k t)")
            dve.wait_ge(slots_ready, 1)
            tt(onehot_slot, slot_iota.unsqueeze(1).to_broadcast([P, J, P]),
               pp.unsqueeze(2).to_broadcast([P, J, P]), ALU.is_equal)
            link(tt(tile_code[:, :, 0, :], tile_iota[:, :].unsqueeze(1).to_broadcast([P, J, TW]),
                    pt.unsqueeze(2).to_broadcast([P, J, TW]), ALU.is_equal))
            link(V.tensor_scalar(tile_code[:, :, 1, :], tile_code[:, :, 0, :], part_iota[:, :], None, ALU.mult))
            tt(tile_code[:, :, 0, :], tile_code[:, :, 0, :], hi_code[:, :].unsqueeze(2).to_broadcast([P, J, TW]),
               ALU.mult).then_inc(codes_ready, 1)

            def shared_sum(g):
                for t in range(g * GT, (g + 1) * GT):
                    dve.wait_ge(down_done, t + 1)
                    tt(x_early[:, t, :], x_early[:, t, :], psum[:, 4 + t % GT, :], ALU.add).then_inc(z_ready, 1)

            shared_sum(0)
            shared_hidden(1)
            dve.wait_ge(dispatch_done, 1)
            link(V.tensor_scalar(code_f[:, :], psum[:, 0, 0:TW], -float(P), float(ASSIGN), ALU.mult, ALU.add))
            link(tt(code_f[:, :], code_f[:, :], psum[:, 0, TW:2 * TW], ALU.add))
            link(V.tensor_copy(to_row[:, :], code_f[:, :]))
            V.tensor_scalar(from_row[:, :], to_row[:, :], TOKENS - 1, None, ALU.bitwise_and).then_inc(tables_ready, 1)
            shared_sum(1)

            def rows_transposed(b, done):
                dve.wait_ge(xgT_done, done)
                V.tensor_copy(xgT[:, b], psum[:, b, :].rearrange("p (c n) -> p c n", c=C)).then_inc(xgT_ready, 1)

            def dve_step(i, b, last=False):
                e = dve.value_load(tile_expert[0:1, bass.ds(i, 1)], min_val=0, max_val=E - 1)
                dve.wait_ge(h_done, i + 1)
                tt(h_sb[:, b], psum[:, 2 + b, 0:2 * INTER].rearrange("p (w n) -> p w n", w=2),
                   ebias[:, bass.ds(e, 1), :, :].rearrange("p u w n -> p (u w) n"), ALU.add).then_inc(h_ready, 1)
                if not last:
                    rows_transposed(1 - b, i + 2)
                dve.wait_ge(s_ready, i + 1)
                tt(g_sb[:, b, :], s_sb[:, b, :], h_sb[:, b, 1, :], ALU.mult).then_inc(g_ready, 1)

            dve.wait_ge(experts_loaded, 16 * EXPERT_LOADS)
            rows_transposed(0, 1)
            pairs = (TILES - 1) // 2
            with dve.Fori(0, pairs) as j:
                for u in range(2):
                    dve_step(j * 2 + u, u)
            dve_step(TILES - 1, 0, last=True)

            def add_rows(g):
                dve.wait_ge(rows_loaded[g], 32)
                if g < EARLY:
                    dve.wait_ge(z_ready, (g + 1) * GT)
                else:
                    dve.wait_ge(x_again_loaded, 16)
                for t in range(g * GT, (g + 1) * GT):
                    acc = x_early[:, t, :] if g < EARLY else x_again[:, t - EARLY * GT, :]
                    for k in range(TOPK):
                        ins = V.scalar_tensor_tensor(out=acc, in0=rows_k[:, g % 2, k, t % GT, :],
                                                     scalar=tops[:, k, t:t + 1], in1=acc,
                                                     op0=ALU.mult, op1=ALU.add)
                        if k == 0:
                            link(ins)
                    if g < EARLY:
                        ins.then_inc(out_ready, 1)
                    else:
                        link(ins)

            def late_sum(g):
                for t in range(g * GT, (g + 1) * GT):
                    dve.wait_ge(down_done, t + 1)
                    acc = x_again[:, t - EARLY * GT, :]
                    tt(acc, acc, psum[:, 4 + t % GT, :], ALU.add).then_inc(z_ready, 1)

            shared_hidden(2)
            add_rows(0)
            add_rows(1)
            add_rows(2)
            late_sum(2)
            shared_hidden(3)
            add_rows(3)
            late_sum(3)


INS = ['x', 'cond_128', 'L0_cond_W0', 'L0_cond_b0', 'L0_cond_W1', 'L0_cond_b1', 'L0_cond_W2', 'L0_cond_b2',
       'L0_cond_weight', 'L0_cond_bias_k', 'L0_ffn_router_w', 'L0_ffn_router_b', 'L0_ffn_router_bias',
       'L0_ffn_ew1', 'L0_ffn_eb1', 'L0_ffn_ew2', 'L0_ffn_eb2', 'L0_ffn_ew3', 'L0_ffn_eb3',
       'L0_ffn_sw1', 'L0_ffn_sb1', 'L0_ffn_sw2', 'L0_ffn_sb2', 'L0_ffn_sw3', 'L0_ffn_sb3']


def kernel(**inputs):
    import numpy as np
    import concourse.bacc as bacc
    from concourse.bass_utils import run_bass_kernel_spmd

    nc = bacc.Bacc("TRN2", target_bir_lowering=False, num_devices=1)
    arrays, args = {}, []
    for name in INS:
        a = np.ascontiguousarray(inputs[name])
        arrays[f"in_{name}"] = a
        args.append(nc.dram_tensor(f"in_{name}", a.shape, mybir.dt.from_np(a.dtype), kind="ExternalInput").ap())
    shape = inputs['x'].shape
    args.append(nc.dram_tensor("out_dram", shape, F32, kind="ExternalOutput").ap())
    adaln_moe_ffn(nc, *args)
    r = run_bass_kernel_spmd(nc, [arrays], core_ids=[0])
    return r.results[0]["out_dram"]
```

```python
from contextlib import ExitStack

import concourse.bass as bass
from concourse import mybir

P = 128
ALU = mybir.AluOpType
ACT = mybir.ActivationFunctionType
AX_X = mybir.AxisListType.X
F32 = mybir.dt.float32
BF16 = mybir.dt.bfloat16
I32 = mybir.dt.int32
U32 = mybir.dt.uint32

MASKED = -1.0e30
TAKEN = -3.0e30


def adaln_moe_ffn(nc, x, cond_pack, router_pack, shared_pack, expert_pack, expert_bias, down_bias, out):
    BS, IN_C, DIM = x.shape
    E, _, EW = expert_pack.shape
    EMB = HID = P
    KMIX = 8
    INTER = EW // (2 * DIM // P + DIM // P)
    SHARED = 2 * INTER
    TOKENS = BS * IN_C
    TOPK = 2
    NGROUPS, GSIZE = 4, E // 4
    NT = TOKENS // P
    C = DIM // P
    BPT = P // IN_C
    KC = KMIX * IN_C // P
    KPC = KMIX // KC
    GT = 4
    NG = NT // GT
    EARLY = NG // 2
    GN = GT * P
    IB = SHARED // P
    ASSIGN = TOKENS * TOPK
    TILES = (ASSIGN + E * (P - 1)) // P
    TW = TILES + 1
    PAIRS = TW // 2
    SURE = ASSIGN // P // 2
    RING = 4

    x_rows = x.rearrange("b c d -> (b c) d")
    out_rows = out.rearrange("b c d -> (b c) d")
    xt_dram = nc.dram_tensor("xt_rows", [TOKENS, DIM], F32, kind="Internal").ap()
    y_dram = nc.dram_tensor("expert_rows", [ASSIGN, DIM], F32, kind="Internal").ap()

    ctx = ExitStack()
    with ctx:
        def sb(name, shape, dt=F32):
            return ctx.enter_context(nc.sbuf_tensor(name, shape, dt))

        def sem(name):
            return ctx.enter_context(nc.semaphore(name))

        wexp = sb("wexp", [P, E, EW])
        ebias = sb("ebias", [P, E, 2, INTER])
        shared_sb = sb("shared_sb", [P, 2 * C * SHARED + IB * DIM])
        sw12 = shared_sb[:, 0:2 * C * SHARED].rearrange("p (w c n) -> p w c n", w=2, c=C)
        sw3_sb = shared_sb[:, 2 * C * SHARED:].rearrange("p (i n) -> p i n", i=IB)
        x_early = sb("x_early", [P, EARLY * GT, DIM])
        late_region = sb("late_region", [P, 16384 // 4])
        xT = sb("xT", [P, NG, C, GN])
        r1 = sb("r1", [P, 8192 // 4])
        xt_sb = sb("xt_sb", [P, 8192 // 4])

        x_late = late_region[:, :].rearrange("p (t d) -> p t d", d=DIM)
        onehot_slot = late_region[:, 0:2048].bitcast(BF16).rearrange("p (j s) -> p j s", s=P)
        temps = late_region[:, 2048:4096].rearrange("p (n f) -> p n f", f=NT * E)
        S, mk, cc, oh1, oh2, t5 = (temps[:, n, :] for n in range(6))
        last_temps = late_region[:, 2048 + 6 * NT * E:4096]
        gate17 = last_temps[:, 0:NT * (E + 1)].rearrange("p (t e) -> p t e", e=E + 1)
        chosen = last_temps[:, 272:272 + 128].bitcast(BF16)
        pos = last_temps[:, 400:432].rearrange("p (k t) -> p k t", k=TOPK)
        pos_i = last_temps[:, 432:464].bitcast(I32).rearrange("p (k t) -> p k t", k=TOPK)
        ptile = last_temps[:, 464:496].rearrange("p (k t) -> p k t", k=TOPK)
        xg = late_region[:, 0:2048].rearrange("p (r d) -> p r d", d=DIM)
        y_sb = late_region[:, 2048:3072].rearrange("p (r d) -> p r d", d=DIM)

        mixT = r1[:, :].rearrange("p (t m) -> p t m", m=P)
        tile_code = r1[:, 0:1536].bitcast(BF16).rearrange("p (j v t) -> p j v t", v=2, t=TW)
        xgT = r1[:, 0:1024].rearrange("p (r c n) -> p r c n", r=2, c=C)
        h_sb = r1[:, 1024:1536].rearrange("p (r w n) -> p r w n", r=2, w=2)
        s_sb = r1[:, 1536:1792].rearrange("p (r n) -> p r n", r=2)
        g_sb = r1[:, 1792:2048].rearrange("p (r n) -> p r n", r=2)

        xt_ring = xt_sb[:, :].rearrange("p (r d) -> p r d", d=DIM)
        gs_sb = xt_sb[:, 0:1024].rearrange("p (i n) -> p i n", i=IB)
        eb3x = xt_sb[0:E + 1, 1024:1536]
        gT_sb = xt_sb[:, 1536:1792].rearrange("p (r n) -> p r n", r=2)

        slot_iota = xt_sb[:, 1792:1792 + P]

        cpool = xT[:, NG - 2, :, :].rearrange("p c n -> p (c n)")
        cpos = [0]

        def early(rows, cols):
            a = cpool[0:rows, cpos[0]:cpos[0] + cols]
            cpos[0] += cols
            return a

        condT, W0_sb, W1_sb, W2_sb = early(P, BS), early(P, HID), early(P, HID), early(P, KMIX)
        b0_sb, b1_sb, b2_sb = early(P, 1), early(P, 1), early(BS, KMIX)
        mix_wT = early(P, KC * (IN_C + 1)).rearrange("p (k o) -> p k o", k=KC)
        cond_in = cpool[:, 0:cpos[0]]
        h1T, h2T = early(P, BS), early(P, BS)
        att, att_e = early(BS, KMIX), early(BS, KMIX)
        att_max, att_sum, att_rec = early(BS, 1), early(BS, 1), early(BS, 1)
        att_rep = early(BS, KMIX * IN_C)
        att_cols = early(P, KC * BS).rearrange("p (k b) -> p k b", k=KC)
        diag32 = early(P, IN_C)
        attK = xT[:, NG - 1, :, :].rearrange("p c n -> p (c n)").rearrange(
            "p (r k b i) -> p r k b i", r=2, k=KC, b=BS // NG)
        gateT = xT[0:E + 1, 0, :, :].rearrange("p c n -> p (c n)")

        wexp_flat = wexp[:, :, :].rearrange("p e n -> p (e n)")
        rows_k = wexp_flat[:, 0:2 * TOPK * GT * DIM].rearrange("p (b k t d) -> p b k t d", b=2, k=TOPK, t=GT)
        x_again = wexp_flat[:, 8192:8192 + 8 * DIM].rearrange("p (t d) -> p t d", d=DIM)

        ident = sb("ident", [P, P])
        before = sb("before", [P, P], BF16)
        ones_bf = sb("ones_bf", [P, P], BF16)
        router_sb = sb("router_sb", [P, C * E + 2 * E + 2 * IB])
        rw_sb = router_sb[:, 0:C * E].rearrange("p (c e) -> p c e", c=C)
        rb_sb = router_sb[:, C * E:C * E + E]
        rbias_sb = router_sb[:, C * E + E:C * E + 2 * E]
        sb12_sb = router_sb[:, C * E + 2 * E:].rearrange("p (w i) -> p w i", w=2)
        mix_bias = sb("mix_bias", [P, NT])
        rev_e = sb("rev_e", [P, E])
        tile_iota = sb("tile_iota", [P, TW])
        part_iota = sb("part_iota", [P, 1])
        hi_code = sb("hi_code", [P, TOPK * NT])
        lower = sb("lower", [P, NGROUPS, NGROUPS])
        restart = sb("restart", [P, NT])
        steps128 = sb("steps128", [P, NT])
        tops = sb("tops", [P, TOPK, NT])
        small = sb("small", [P, 4, NT])
        count = sb("count", [P, 4, E])
        pslot = sb("pslot", [P, TOPK, NT])
        tile_expert = sb("tile_expert", [P, TW], I32)
        tile_counts = sb("tile_counts", [P, 3], I32)
        count_f = sb("count_f", [P, 1])
        code_f = sb("code_f", [P, TW])
        to_row = sb("to_row", [P, TW], I32)
        from_row = sb("from_row", [P, TW + RING], I32)
        to_slot = sb("to_slot", [P, RING], I32)
        from_slot = sb("from_slot", [P, RING], I32)

        psum = ctx.enter_context(nc.psum_tensor("psum", [P, 8, 512], F32))

        cond_loaded = sem("cond_loaded")
        x_loaded = [sem(f"x_loaded{g}") for g in range(NG)]
        router_loaded = sem("router_loaded")
        shared_loaded = sem("shared_loaded")
        experts_loaded = sem("experts_loaded")
        eb3_loaded = sem("eb3_loaded")
        consts_ready = sem("consts_ready")
        ident_ready = sem("ident_ready")
        diag_ready = sem("diag_ready")
        slots_ready = sem("slots_ready")
        pool_chain = sem("pool_chain")
        dve_chain = sem("dve_chain")
        act_chain = sem("act_chain")
        pe_cond = sem("pe_cond")
        dve_cond = sem("dve_cond")
        act_cond = sem("act_cond")
        attK_ready = sem("attK_ready")
        mix_done = sem("mix_done")
        mix_copied = sem("mix_copied")
        xt_done = sem("xt_done")
        xt_ready = sem("xt_ready")
        xt_stored = [sem(f"xt_stored{r}") for r in range(RING)]
        xtT_done = sem("xtT_done")
        xT_ready = sem("xT_ready")
        logits_done = sem("logits_done")
        shifted_ready = sem("shifted_ready")
        exp_ready = sem("exp_ready")
        gates_ready = sem("gates_ready")
        gateT_done = sem("gateT_done")
        gateT_ready = sem("gateT_ready")
        chosen_ready = sem("chosen_ready")
        ranks_done = sem("ranks_done")
        ranks_read = sem("ranks_read")
        codes_ready = sem("codes_ready")
        dispatch_done = sem("dispatch_done")
        tables_ready = sem("tables_ready")
        up_done = sem("up_done")
        up_silu = sem("up_silu")
        up_ready = sem("up_ready")
        down_done = sem("down_done")
        z_ready = sem("z_ready")
        from_copied = sem("from_copied")
        to_copied = sem("to_copied")
        pool_held = sem("pool_held")
        xg_loaded = [sem(f"xg_loaded{r}") for r in range(RING)]
        xgT_done = sem("xgT_done")
        xgT_ready = sem("xgT_ready")
        h_done = sem("h_done")
        h_ready = sem("h_ready")
        s_ready = sem("s_ready")
        g_ready = sem("g_ready")
        gT_done = sem("gT_done")
        gT_ready = sem("gT_ready")
        y_done = sem("y_done")
        y_ready = sem("y_ready")
        scattered = [sem(f"scattered{r}") for r in range(2)]
        x_again_loaded = sem("x_again_loaded")
        rows_loaded = [sem(f"rows_loaded{g}") for g in range(NG)]
        out_ready = sem("out_ready")
        out_stored = sem("out_stored")

        EXPERT_LOADS = E + 1
        MIX_AT = {2 * g - 1: g for g in range(1, NG)}

        block = ctx.enter_context(nc.Block())

        def x_tile(t):
            return x_early[:, t, :] if t < EARLY * GT else x_late[:, t - EARLY * GT, :]

        def xT_tile(t, c):
            return xT[:, t // GT, c, (t % GT) * P:(t % GT + 1) * P]

        def store_group(sp, g):
            for t in range(g * GT, (g + 1) * GT):
                sp.wait_ge(*((out_ready, t + 1) if t < EARLY * GT else (z_ready, t + 1)))
                src = x_early[:, t, :] if t < EARLY * GT else x_again[:, t - EARLY * GT, :]
                sp.dma_start(out_rows[t * P:(t + 1) * P, :], src).then_inc(out_stored, 16)

        @block.sync
        def _(sp):
            sp.dma_start(cond_in, cond_pack).then_inc(cond_loaded, 16)
            for g in range(NG):
                dst = x_early[:, g * GT:(g + 1) * GT, :] if g < EARLY else \
                    x_late[:, (g - EARLY) * GT:(g - EARLY + 1) * GT, :]
                sp.dma_start(dst, x_rows[g * GN:(g + 1) * GN, :].rearrange("(t p) d -> p t d", p=P)
                             ).then_inc(x_loaded[g], 16)
                if g == 0:
                    sp.dma_start(router_sb[:, :], router_pack).then_inc(router_loaded, 16)
            sp.dma_start(shared_sb[:, :], shared_pack).then_inc(shared_loaded, 16)
            sp.dma_start(ebias[:, :, :, :].rearrange("p e w n -> p (e w n)"),
                         expert_bias.to_broadcast([P, E * 2 * INTER])).then_inc(experts_loaded, 16)
            for t in range(NT):
                sp.wait_ge(xt_ready, t + 1)
                sp.dma_start(xt_dram[t * P:(t + 1) * P, :], xt_ring[:, t % RING, :]
                             ).then_inc(xt_stored[t % RING], 16)
                sp.dma_start(wexp[:, t, :], expert_pack[t]).then_inc(experts_loaded, 16)
            for r in range(RING):
                sp.wait_ge(xt_stored[r], 16 * (NT // RING))
            sp.wait_ge(xtT_done, NT)
            sp.dma_start(eb3x, down_bias).then_inc(eb3_loaded, 16)
            sp.wait_ge(tables_ready, 1)
            tiles = sp.value_load(tile_counts[0:1, 1:2], min_val=2 * SURE, max_val=2 * PAIRS)
            sp.wait_ge(y_done, tiles)
            sp.dma_start(x_again[:, :, :], x_rows[EARLY * GN:NG * GN, :].rearrange("(t p) d -> p t d", p=P)
                         ).then_inc(x_again_loaded, 16)
            for r in range(2):
                sp.wait_ge(scattered[r], tiles * 8)
            for g in range(NG):
                if g >= 2:
                    sp.wait_ge(out_ready, (g - 1) * GT)
                for k in range(TOPK):
                    src = y_dram[k * TOKENS + g * GN:k * TOKENS + (g + 1) * GN, :]
                    sp.dma_start(rows_k[:, g % 2, k], src.rearrange("(t p) d -> p t d", p=P)
                                 ).then_inc(rows_loaded[g], 16)
                if g >= 1:
                    store_group(sp, g - 1)
            store_group(sp, NG - 1)
            sp.wait_ge(out_stored, 16 * NT)

        @block.gpsimd
        def _(pool):
            n = [0]

            def link(ins):
                n[0] += 1
                ins.then_inc(pool_chain, 1)
                pool.wait_ge(pool_chain, n[0])

            link(nc.gpsimd.memset(ident[:, :], 0.0))
            nc.gpsimd.affine_select(out=ident[:, :], in_=ident[:, :], compare_op=ALU.not_equal, fill=1.0,
                                    base=0, pattern=[[-1, P]], channel_multiplier=1).then_inc(ident_ready, 1)
            link(nc.gpsimd.memset(diag32[:, :], 0.0))
            for b in range(BPT):
                link(nc.gpsimd.affine_select(out=diag32[:, :], in_=diag32[:, :], compare_op=ALU.not_equal,
                                             fill=1.0, base=-IN_C * b, pattern=[[-1, IN_C]],
                                             channel_multiplier=1))
            nc.gpsimd.memset(r1[:, :], 0.0).then_inc(diag_ready, 1)
            link(nc.gpsimd.memset(ones_bf[:, :], 1.0))
            link(nc.gpsimd.affine_select(out=before[:, :], in_=ones_bf[:, :], compare_op=ALU.is_gt, fill=0.0,
                                         base=0, pattern=[[1, P]], channel_multiplier=-1))
            for dst, pattern, base, mult in (
                    (rev_e[:, :], [[-1, E]], E, 0),
                    (tile_iota[:, :], [[1, TW]], 0, 0), (part_iota[:, :], [[1, 1]], 0, 1),
                    (hi_code[:, :], [[-1, TOPK * NT]], TOPK * NT, 0),
                    (restart[:, :], [[1, NT]], 0, 0), (steps128[:, :], [[P, NT]], 0, 0),
                    (lower[:, :, :], [[1, NGROUPS], [-1, NGROUPS]], 0, 0)):
                link(nc.gpsimd.iota(dst, pattern=pattern, base=base, channel_multiplier=mult,
                                    allow_small_or_imprecise_dtypes=True))
            link(nc.gpsimd.tensor_scalar(restart[:, :], restart[:, :], 1.0, None, ALU.min))
            link(nc.gpsimd.tensor_scalar(lower[:, :, :], lower[:, :, :], 0.0, None, ALU.is_gt))
            nc.gpsimd.memset(to_slot[:, :], 0).then_inc(consts_ready, 1)

            pool.wait_ge(xtT_done, NT)
            for r in range(RING):
                pool.wait_ge(xt_stored[r], 16 * (NT // RING))
            nc.gpsimd.iota(slot_iota, pattern=[[1, P]], base=0, channel_multiplier=0,
                           allow_small_or_imprecise_dtypes=True).then_inc(slots_ready, 1)
            pool.wait_ge(tables_ready, 1)

            def hold(semaphore, value):
                pool.wait_ge(semaphore, value)
                pool.sem_inc(pool_held, 1)

            def gather(i, slot):
                nc.gpsimd.tensor_copy(from_slot[:, slot:slot + 1], from_row[:, bass.ds(i, 1)]
                                      ).then_inc(from_copied, 1)
                hold(from_copied, i + 1)
                nc.gpsimd.indirect_dma_start(
                    out=xg[:, slot, :], out_offset=None, in_=xt_dram[:, :],
                    in_offset=bass.IndirectOffsetOnAxis(ap=from_slot[:, slot:slot + 1].bitcast(U32), axis=0),
                ).then_inc(xg_loaded[slot], 16)

            def scatter(i, slot):
                hold(y_ready, i + 1)
                nc.gpsimd.tensor_copy(to_slot[:, slot:slot + 1], to_row[:, bass.ds(i, 1)]
                                      ).then_inc(to_copied, 1)
                hold(to_copied, i + 1)
                nc.gpsimd.indirect_dma_start(
                    out=y_dram[:, :],
                    out_offset=bass.IndirectOffsetOnAxis(ap=to_slot[:, slot:slot + 1].bitcast(U32), axis=0),
                    in_=y_sb[:, slot, :], in_offset=None, bounds_check=ASSIGN - 1, oob_is_err=False,
                ).then_inc(scattered[slot], 16)

            def gather_ahead(p, q):
                for u in range(2):
                    hold(xgT_done, p * 2 + u + 1)
                    gather(p * 2 + RING + u, 2 * q + u)

            def pool_pair(p, q, first=False, ahead=True):
                if not first:
                    scatter(p * 2 - 1, 1)
                if ahead:
                    gather_ahead(p, q)
                scatter(p * 2, 0)

            pairs = pool.value_load(tile_counts[0:1, 0:1], min_val=SURE, max_val=PAIRS)
            tiles = pool.value_load(tile_counts[0:1, 1:2], min_val=2 * SURE, max_val=2 * PAIRS)
            for i in range(RING):
                gather(i, i)
            pool_pair(0, 0, first=True)
            pool_pair(1, 1)
            with pool.Fori(0, (SURE - 4) // 2) as j:
                for q in range(2):
                    pool_pair(j * 2 + 2 + q, q)
            for p in (SURE - 2, SURE - 1):
                scatter(p * 2 - 1, 1)
                with pool.If(pairs > p + 2):
                    gather_ahead(p, p % 2)
                scatter(p * 2, 0)
            with pool.Fori(0, (PAIRS - SURE) // 2) as j:
                for q in range(2):
                    p = j * 2 + SURE + q
                    with pool.If(pairs > p):
                        scatter(p * 2 - 1, 1)
                        with pool.If(pairs > p + 2):
                            gather_ahead(p, q)
                        scatter(p * 2, 0)
            scatter(tiles - 1, 1)

        @block.tensor
        def _(pe):
            def mm(dst, lhsT, rhs, start=True, stop=True):
                return nc.tensor.matmul(dst, lhsT, rhs, start=start, stop=stop)

            pe.wait_ge(cond_loaded, 16)
            mm(psum[:, 2, 0:BS], W0_sb, condT).then_inc(pe_cond, 1)
            pe.wait_ge(act_cond, 1)
            mm(psum[:, 3, 0:BS], W1_sb, h1T).then_inc(pe_cond, 1)
            pe.wait_ge(act_cond, 2)
            mm(psum[0:BS, 4, 0:KMIX], h2T, W2_sb).then_inc(pe_cond, 1)
            pe.wait_ge(ident_ready, 1)
            pe.wait_ge(dve_cond, 2)
            for k in range(KC):
                last = nc.tensor.transpose(psum[:, 5, k * BS:(k + 1) * BS], att_rep[:, k * P:(k + 1) * P],
                                           ident[0:BS, 0:BS])
            last.then_inc(pe_cond, 1)

            def mix(g):
                pe.wait_ge(attK_ready, g + 1)
                for t in range(GT):
                    for k in range(KC):
                        last = mm(psum[:, 6 + g % 2, t * 33:t * 33 + 33],
                                  attK[:, g % 2, k, t * BPT:(t + 1) * BPT, :].rearrange("p b i -> p (b i)"),
                                  mix_wT[:, k, :], start=(k == 0), stop=(k == KC - 1))
                last.then_inc(mix_done, 1)

            mix(0)
            for s in range(NT + 2):
                if s < NT:
                    if s % GT == 0:
                        pe.wait_ge(x_loaded[s // GT], 16)
                        pe.wait_ge(mix_copied, s // GT + 1)
                    if s >= 2:
                        pe.wait_ge(xt_ready, s - 1)
                    mm(psum[:, s % 2, :], mixT[:, s, :], x_tile(s)).then_inc(xt_done, 1)
                if 1 <= s <= NT:
                    t = s - 1
                    pe.wait_ge(xt_ready, t + 1)
                    if t >= 2:
                        pe.wait_ge(xT_ready, t - 1)
                    for c in range(C):
                        last = nc.tensor.transpose(psum[:, 2 + t % 2, c * P:(c + 1) * P],
                                                   xt_ring[:, t % RING, c * P:(c + 1) * P], ident[:, :])
                    last.then_inc(xtT_done, 1)
                if s >= 2:
                    t = s - 2
                    if t == 0:
                        pe.wait_ge(router_loaded, 16)
                    pe.wait_ge(xT_ready, t + 1)
                    for c in range(C):
                        last = mm(psum[:, 4, t * E:(t + 1) * E], xT_tile(t, c), rw_sb[:, c, :],
                                  start=(c == 0), stop=(c == C - 1))
                if s in MIX_AT:
                    mix(MIX_AT[s])
            last.then_inc(logits_done, 1)

            def shared_up(g):
                for i in range(IB):
                    n = g * IB + i
                    if n >= 2:
                        pe.wait_ge(up_ready, n - 1)
                    if n == 3:
                        pe.wait_ge(ranks_read, 1)
                    for w in range(2):
                        for c in range(C):
                            last = mm(psum[:, 2 * i + w, :], sw12[:, w, c, i * P:(i + 1) * P], xT[:, g, c, :],
                                      start=(c == 0), stop=(c == C - 1))
                    last.then_inc(up_done, 1)

            def shared_down(g):
                pe.wait_ge(up_ready, IB * (g + 1))
                for t in range(g * GT, (g + 1) * GT):
                    if t >= GT:
                        pe.wait_ge(z_ready, t - GT + 1)
                    else:
                        pe.wait_ge(gateT_ready, t + 1)
                    bank = psum[:, 4 + t % GT, :]
                    for i in range(IB):
                        mm(bank, gs_sb[:, i, (t % GT) * P:(t % GT + 1) * P], sw3_sb[:, i, :],
                           start=(i == 0), stop=False)
                    if t == 0:
                        pe.wait_ge(gateT_ready, NG)
                        pe.wait_ge(eb3_loaded, 16)
                    mm(bank, gateT[:, t * P:(t + 1) * P], eb3x, start=False, stop=True).then_inc(down_done, 1)

            pe.wait_ge(shared_loaded, 16)
            shared_up(0)
            pe.wait_ge(gates_ready, 1)
            for t in range(NT):
                last = nc.tensor.transpose(psum[0:E + 1, 4 + t // GT, (t % GT) * P:(t % GT + 1) * P],
                                           gate17[:, t, :], ident[:, :])
                if t % GT == GT - 1:
                    last.then_inc(gateT_done, 1)
            pe.wait_ge(chosen_ready, 1)
            pe.wait_ge(up_ready, 2)
            mm(psum[:, 3, 0:NT * E], before[:, :], chosen)
            mm(psum[:, 3, NT * E:2 * NT * E], ones_bf[:, :], chosen).then_inc(ranks_done, 1)
            shared_down(0)
            shared_up(1)
            pe.wait_ge(codes_ready, 1)
            pe.wait_ge(up_ready, 2 * IB)
            for j in range(TOPK * NT):
                last = mm(psum[:, 0, 0:2 * TW], onehot_slot[:, j, :],
                          tile_code[:, j, :, :].rearrange("p v t -> p (v t)"),
                          start=(j == 0), stop=(j == TOPK * NT - 1))
            last.then_inc(dispatch_done, 1)
            shared_down(1)

            pe.wait_ge(experts_loaded, 16 * EXPERT_LOADS)
            pe.wait_ge(z_ready, EARLY * GT)
            pe.wait_ge(tables_ready, 1)

            def rows_transposed(b, slot, loaded):
                pe.wait_ge(xg_loaded[slot], loaded)
                for c in range(C):
                    last = nc.tensor.transpose(psum[:, b, c * P:(c + 1) * P], xg[:, slot, c * P:(c + 1) * P],
                                               ident[:, :])
                last.then_inc(xgT_done, 1)

            def up(b, e, half):
                for c in range(half * C // 2, (half + 1) * C // 2):
                    w = wexp[:, bass.ds(e, 1), 0:2 * C * INTER].rearrange("p u (w c n) -> p (u w) c n", w=2, c=C)
                    last = mm(psum[:, 2 + b, 0:2 * INTER].rearrange("p (w n) -> p w n", w=2), xgT[:, b, c, :],
                              w[:, :, c, :], start=(c == 0), stop=(c == C - 1))
                return last

            def hidden_transposed(b, ready):
                pe.wait_ge(g_ready, ready)
                nc.tensor.transpose(psum[:, 4 + b, 0:P], g_sb[:, b, :], ident[:, :]).then_inc(gT_done, 1)

            def down(b, e, ready, freed):
                pe.wait_ge(gT_ready, ready)
                if freed is not None:
                    pe.wait_ge(y_ready, freed)
                mm(psum[:, 6 + b, :], gT_sb[:, b, :],
                   wexp[:, bass.ds(e, 1), 2 * C * INTER:].rearrange("p u n -> p (u n)")).then_inc(y_done, 1)

            def expert_of(i):
                return pe.value_load(tile_expert[0:1, bass.ds(i, 1)], min_val=0, max_val=E - 1)

            def pe_pair(p, q, loaded):
                first, second = isinstance(p, int) and p == 0, isinstance(p, int) and p == 1
                rows_transposed(0, 2 * q, loaded)
                if not first:
                    hidden_transposed(1, p * 2)
                rows_transposed(1, 2 * q + 1, loaded)
                if not first:
                    down(1, expert_of(p * 2 - 1), p * 2, None if second else p * 2 - 2)
                ea = expert_of(p * 2)
                pe.wait_ge(xgT_ready, p * 2 + 1)
                up(0, ea, 0)
                up(0, ea, 1).then_inc(h_done, 1)
                eb = expert_of(p * 2 + 1)
                pe.wait_ge(xgT_ready, p * 2 + 2)
                up(1, eb, 0)
                hidden_transposed(0, p * 2 + 1)
                up(1, eb, 1).then_inc(h_done, 1)
                down(0, expert_of(p * 2), p * 2 + 1, None if first else p * 2 - 1)

            pe_pair(0, 0, 16)
            pe_pair(1, 1, 16)
            with pe.Fori(0, (SURE - 2) // 2) as j:
                for q in range(2):
                    pe_pair(j * 2 + 2 + q, q, j * 16 + 32)
            pairs = pe.value_load(tile_counts[0:1, 0:1], min_val=SURE, max_val=PAIRS)
            with pe.Fori(0, (PAIRS - SURE) // 2) as j:
                for q in range(2):
                    p = j * 2 + SURE + q
                    with pe.If(pairs > p):
                        pe_pair(p, q, j * 16 + 16 * (SURE // 2 + 1))
            tiles = pe.value_load(tile_counts[0:1, 1:2], min_val=2 * SURE, max_val=2 * PAIRS)
            hidden_transposed(1, tiles)
            tiles_less_2 = pe.value_load(tile_counts[0:1, 2:3], min_val=2 * SURE - 2, max_val=2 * PAIRS - 2)
            down(1, expert_of(tiles - 1), tiles, tiles_less_2)

            shared_up(2)
            pe.wait_ge(y_ready, tiles)
            shared_down(2)
            shared_up(3)
            shared_down(3)

        @block.scalar
        def _(act):
            act.wait_ge(cond_loaded, 16)
            act.wait_ge(pe_cond, 1)
            nc.scalar.activation(h1T, psum[:, 2, 0:BS], ACT.Gelu, bias=b0_sb).then_inc(act_cond, 1)
            act.wait_ge(pe_cond, 2)
            nc.scalar.activation(h2T, psum[:, 3, 0:BS], ACT.Gelu, bias=b1_sb).then_inc(act_cond, 1)
            act.wait_ge(dve_cond, 1)
            nc.scalar.activation(att_e, att, ACT.Exp, accum_out=att_sum).then_inc(act_cond, 1)
            for t in range(NT):
                if t % GT == 0:
                    act.wait_ge(mix_copied, t // GT + 1)
                act.wait_ge(xt_done, t + 1)
                if t >= RING:
                    act.wait_ge(xt_stored[t % RING], 16 * (t // RING))
                    act.wait_ge(xtT_done, t - RING + 1)
                nc.scalar.activation(xt_ring[:, t % RING, :], psum[:, t % 2, :], ACT.Identity,
                                     bias=mix_bias[:, t:t + 1]).then_inc(xt_ready, 1)
            act.wait_ge(shifted_ready, 1)
            nc.scalar.activation(mk, S, ACT.Exp).then_inc(exp_ready, 1)

            def shared_silu(g):
                for i in range(IB):
                    act.wait_ge(up_done, g * IB + i + 1)
                    if g >= 1:
                        act.wait_ge(down_done, g * GT)
                    nc.scalar.activation(gs_sb[:, i, :], psum[:, 2 * i, :], ACT.Silu, bias=sb12_sb[:, 0, i:i + 1]
                                         ).then_inc(up_silu, 1)

            act.wait_ge(router_loaded, 16)
            act.wait_ge(xtT_done, NT)
            for r in range(RING):
                act.wait_ge(xt_stored[r], 16 * (NT // RING))
            shared_silu(0)
            for q in range(NG):
                act.wait_ge(gateT_done, q + 1)
                nc.scalar.activation(gateT[:, q * GN:(q + 1) * GN], psum[0:E + 1, 4 + q, :], ACT.Copy
                                     ).then_inc(gateT_ready, 1)
            shared_silu(1)

            def hidden_transposed(b, done):
                act.wait_ge(gT_done, done)
                nc.scalar.activation(gT_sb[:, b, :], psum[:, 4 + b, 0:P], ACT.Copy).then_inc(gT_ready, 1)

            def silu(b, done):
                act.wait_ge(h_ready, done)
                nc.scalar.activation(s_sb[:, b, :], h_sb[:, b, 0, :], ACT.Silu).then_inc(s_ready, 1)

            def result(b, done, freed):
                act.wait_ge(y_done, done)
                if freed is not None:
                    act.wait_ge(scattered[b], freed)
                nc.scalar.activation(y_sb[:, b, :], psum[:, 6 + b, :], ACT.Copy).then_inc(y_ready, 1)

            def act_pair(p):
                first, second = isinstance(p, int) and p == 0, isinstance(p, int) and p == 1
                if not first:
                    hidden_transposed(1, p * 2)
                    result(1, p * 2, None if second else p * 16 - 16)
                silu(0, p * 2 + 1)
                hidden_transposed(0, p * 2 + 1)
                silu(1, p * 2 + 2)
                result(0, p * 2 + 1, None if first else p * 16)

            act_pair(0)
            act_pair(1)
            with act.Fori(2, SURE) as p:
                act_pair(p)
            act.wait_ge(tables_ready, 1)
            pairs = act.value_load(tile_counts[0:1, 0:1], min_val=SURE, max_val=PAIRS)
            with act.Fori(SURE, PAIRS) as p:
                with act.If(pairs > p):
                    act_pair(p)
            tiles = act.value_load(tile_counts[0:1, 1:2], min_val=2 * SURE, max_val=2 * PAIRS)
            hidden_transposed(1, tiles)
            tiles_less_2 = act.value_load(tile_counts[0:1, 2:3], min_val=2 * SURE - 2, max_val=2 * PAIRS - 2)
            result(1, tiles, tiles_less_2 * 8)
            shared_silu(2)
            shared_silu(3)

        @block.vector
        def _(dve):
            n = [0]

            def link(ins):
                n[0] += 1
                ins.then_inc(dve_chain, 1)
                dve.wait_ge(dve_chain, n[0])

            def tt(dst, a, b, op):
                return nc.vector.tensor_tensor(dst, a, b, op)

            V = nc.vector
            dve.wait_ge(pe_cond, 3)
            dve.wait_ge(cond_loaded, 16)
            link(tt(att, psum[0:BS, 4, 0:KMIX], b2_sb, ALU.add))
            link(V.tensor_reduce(att_max, att, AX_X, ALU.max))
            V.tensor_scalar(att, att, att_max, None, ALU.subtract).then_inc(dve_cond, 1)
            dve.wait_ge(act_cond, 3)
            link(V.reciprocal(att_rec, att_sum))
            V.tensor_scalar(att_rep.rearrange("b (k i) -> b k i", k=KMIX),
                            att_e.unsqueeze(2).to_broadcast([BS, KMIX, IN_C]), att_rec, None, ALU.mult
                            ).then_inc(dve_cond, 1)
            dve.wait_ge(pe_cond, 4)
            link(V.tensor_copy(att_cols, psum[:, 5, 0:KC * BS].rearrange("p (k b) -> p k b", k=KC)))
            dve.wait_ge(diag_ready, 1)
            GB = BS // NG

            def spread(g):
                if g >= 2:
                    dve.wait_ge(mix_done, g - 1)
                for k in range(KC):
                    last = tt(attK[:, g % 2, k], att_cols[:, k, g * GB:(g + 1) * GB].unsqueeze(2)
                              .to_broadcast([P, GB, IN_C]),
                              diag32.unsqueeze(1).to_broadcast([P, GB, IN_C]), ALU.mult)
                last.then_inc(attK_ready, 1)

            def mixed(g):
                dve.wait_ge(mix_done, g + 1)
                blocks = psum[:, 6 + g % 2, 0:GT * 33].rearrange("p (t o) -> p t o", o=33)
                V.tensor_copy(mix_bias[:, g * GT:(g + 1) * GT], blocks[:, :, IN_C])
                for b in range(BPT):
                    rows = slice(b * IN_C, (b + 1) * IN_C)
                    last = V.tensor_copy(mixT[rows, g * GT:(g + 1) * GT, b * IN_C:(b + 1) * IN_C],
                                         blocks[rows, :, 0:IN_C])
                last.then_inc(mix_copied, 1)

            spread(0)
            spread(1)
            mixed(0)
            for t in range(NT):
                dve.wait_ge(xtT_done, t + 1)
                V.tensor_copy(xT[:, t // GT, :, (t % GT) * P:(t % GT + 1) * P],
                              psum[:, 2 + t % 2, :].rearrange("p (c n) -> p c n", c=C)).then_inc(xT_ready, 1)
                if t in MIX_AT:
                    mixed(MIX_AT[t])
                    if MIX_AT[t] + 1 < NG:
                        spread(MIX_AT[t] + 1)

            def te(a):
                return a.rearrange("p (t e) -> p t e", e=E)

            def over_e(a):
                return a.unsqueeze(2).to_broadcast([P, NT, E])

            def over_t(a):
                return a.unsqueeze(1).to_broadcast([P, NT, E])

            dve.wait_ge(logits_done, 1)
            dve.wait_ge(router_loaded, 16)
            dve.wait_ge(consts_ready, 1)
            link(tt(te(S), te(psum[:, 4, 0:NT * E]), over_t(rb_sb[:, :]), ALU.add))
            link(V.tensor_reduce(small[:, 0, :], te(S), AX_X, ALU.max))
            tt(te(S), te(S), over_e(small[:, 0, :]), ALU.subtract).then_inc(shifted_ready, 1)
            dve.wait_ge(exp_ready, 1)
            link(V.tensor_reduce(small[:, 0, :], te(mk), AX_X, ALU.add))
            link(V.reciprocal(small[:, 1, :], small[:, 0, :]))
            link(tt(te(S), te(mk), over_e(small[:, 1, :]), ALU.mult))
            link(tt(te(S), te(S), over_t(rbias_sb[:, :]), ALU.add))

            gmax = cc[:, 0:NT * NGROUPS]
            link(V.tensor_reduce(gmax, S.rearrange("p (n s) -> p n s", s=GSIZE), AX_X, ALU.max))
            gm = gmax.rearrange("p (t g) -> p t g", g=NGROUPS)
            other = gm.unsqueeze(2).to_broadcast([P, NT, NGROUPS, NGROUPS])
            own = gm.unsqueeze(3).to_broadcast([P, NT, NGROUPS, NGROUPS])

            def tgg(a):
                return a.rearrange("p (t g h) -> p t g h", g=NGROUPS, h=NGROUPS)

            tt(tgg(oh1), other, own, ALU.is_gt)
            link(tt(tgg(oh2), other, own, ALU.is_equal))
            link(tt(tgg(oh2), tgg(oh2), lower[:, :, :].unsqueeze(1).to_broadcast([P, NT, NGROUPS, NGROUPS]),
                    ALU.mult))
            link(tt(oh1, oh1, oh2, ALU.add))
            rank = t5[:, 0:NT * NGROUPS]
            keep = t5[:, NT * NGROUPS:2 * NT * NGROUPS]
            penalty = t5[:, 2 * NT * NGROUPS:3 * NT * NGROUPS]
            link(V.tensor_reduce(rank, oh1.rearrange("p (n h) -> p n h", h=NGROUPS), AX_X, ALU.add))
            V.tensor_scalar(keep, rank, 1.5, None, ALU.is_lt)
            link(V.tensor_scalar(penalty, rank, 1.5, MASKED, ALU.is_ge, ALU.mult))

            def per_group(a):
                return a.unsqueeze(2).to_broadcast([P, NT * NGROUPS, GSIZE])

            def ns(a):
                return a.rearrange("p (n s) -> p n s", s=GSIZE)

            link(tt(ns(mk), ns(S), per_group(keep), ALU.mult))
            link(tt(ns(mk), ns(mk), per_group(penalty), ALU.add))

            for k, oh in enumerate((oh1, oh2)):
                link(V.tensor_reduce(tops[:, k, :], te(mk), AX_X, ALU.max))
                link(tt(te(cc), te(mk), over_e(tops[:, k, :]), ALU.is_equal))
                link(tt(te(cc), te(cc), over_t(rev_e[:, :]), ALU.mult))
                link(V.tensor_reduce(small[:, 0, :], te(cc), AX_X, ALU.max))
                link(tt(te(oh), te(cc), over_e(small[:, 0, :]), ALU.is_equal))
                if k == 0:
                    link(V.scalar_tensor_tensor(out=mk, in0=oh, scalar=TAKEN, in1=mk, op0=ALU.mult, op1=ALU.add))
            tt(chosen, oh1, oh2, ALU.add).then_inc(chosen_ready, 1)
            V.memset(gate17[:, :, E:E + 1], 1.0)
            tt(te(S), te(oh1), over_e(tops[:, 0, :]), ALU.mult)
            link(tt(te(cc), te(oh2), over_e(tops[:, 1, :]), ALU.mult))
            tt(gate17[:, :, 0:E], te(S), te(cc), ALU.add).then_inc(gates_ready, 1)

            def shared_hidden(g):
                for i in range(IB):
                    dve.wait_ge(up_silu, g * IB + i + 1)
                    V.scalar_tensor_tensor(out=gs_sb[:, i, :], in0=psum[:, 2 * i + 1, :],
                                           scalar=sb12_sb[:, 1, i:i + 1], in1=gs_sb[:, i, :],
                                           op0=ALU.add, op1=ALU.mult).then_inc(up_ready, 1)

            shared_hidden(0)

            dve.wait_ge(ranks_done, 1)
            tot, incl, excl = S, mk, cc
            cnt, ntile, end, base = (count[:, q, :] for q in range(4))

            def et(a):
                return a.rearrange("p (e t) -> p e t", t=NT)

            link(V.tensor_copy(et(tot), te(psum[:, 3, NT * E:2 * NT * E]).rearrange("p t e -> p e t")))
            link(V.tensor_copy(et(t5), restart[:, :].unsqueeze(1).to_broadcast([P, E, NT])))
            link(V.tensor_tensor_scan(incl, t5, tot, 0.0, ALU.mult, ALU.add))
            tt(excl, incl, tot, ALU.subtract)
            link(V.tensor_copy(cnt, et(incl)[:, :, NT - 1]))
            link(tt(et(t5), cnt.unsqueeze(2).to_broadcast([P, E, NT]),
                    steps128[:, :].unsqueeze(1).to_broadcast([P, E, NT]), ALU.is_gt))
            link(V.tensor_reduce(ntile, et(t5), AX_X, ALU.add))
            link(V.memset(small[:, 2, :], 1.0))
            link(V.tensor_tensor_scan(end, small[:, 2, :], ntile, 0.0, ALU.mult, ALU.add))
            link(tt(base, end, ntile, ALU.subtract))
            link(V.tensor_scalar(base, base, float(P), None, ALU.mult))
            tt(te(S), te(psum[:, 3, 0:NT * E]), et(excl).rearrange("p e t -> p t e"), ALU.add
               ).then_inc(ranks_read, 1)
            dve.wait_ge(ranks_read, 1)
            link(tt(te(S), te(S), over_t(base), ALU.add))
            for k, oh in enumerate((oh1, oh2)):
                link(tt(mk, oh, S, ALU.mult))
                link(V.tensor_reduce(pos[:, k, :], te(mk), AX_X, ALU.add))
            cmp = late_region[:, 2048:2048 + TW * E].rearrange("p (t e) -> p t e", e=E)
            link(tt(cmp, end.unsqueeze(1).to_broadcast([P, TW, E]),
                    tile_iota[:, :].unsqueeze(2).to_broadcast([P, TW, E]), ALU.is_le))
            link(V.tensor_reduce(code_f[:, :], cmp, AX_X, ALU.add))
            link(V.tensor_scalar(tile_expert[:, :], code_f[:, :], float(E - 1), None, ALU.min))
            link(V.tensor_copy(tile_counts[:, 0:1], end[:, E - 1:E]))
            link(V.tensor_scalar(count_f[:, :], tile_counts[:, 0:1], 1.0, None, ALU.add))
            link(V.tensor_copy(tile_counts[:, 0:1], count_f[:, :]))
            link(V.tensor_scalar(tile_counts[:, 0:1], tile_counts[:, 0:1], 1, None, ALU.arith_shift_right))
            V.tensor_scalar(tile_counts[:, 1:2], tile_counts[:, 0:1], 2.0, None, ALU.mult)
            V.tensor_scalar(tile_counts[:, 2:3], tile_counts[:, 0:1], 2.0, -2.0, ALU.mult, ALU.add)
            link(V.tensor_copy(pos_i[:, :, :], pos[:, :, :]))
            link(V.tensor_scalar(pos_i[:, :, :], pos_i[:, :, :], 7, None, ALU.arith_shift_right))
            link(V.tensor_copy(ptile[:, :, :], pos_i[:, :, :]))
            link(V.scalar_tensor_tensor(out=pslot[:, :, :], in0=ptile[:, :, :], scalar=-float(P),
                                        in1=pos[:, :, :], op0=ALU.mult, op1=ALU.add))
            J = TOPK * NT
            pt = ptile[:, :, :].rearrange("p k t -> p (k t)")
            pp = pslot[:, :, :].rearrange("p k t -> p (k t)")
            dve.wait_ge(slots_ready, 1)
            tt(onehot_slot, slot_iota.unsqueeze(1).to_broadcast([P, J, P]),
               pp.unsqueeze(2).to_broadcast([P, J, P]), ALU.is_equal)
            link(tt(tile_code[:, :, 0, :], tile_iota[:, :].unsqueeze(1).to_broadcast([P, J, TW]),
                    pt.unsqueeze(2).to_broadcast([P, J, TW]), ALU.is_equal))
            link(V.tensor_scalar(tile_code[:, :, 1, :], tile_code[:, :, 0, :], part_iota[:, :], None, ALU.mult))
            tt(tile_code[:, :, 0, :], tile_code[:, :, 0, :], hi_code[:, :].unsqueeze(2).to_broadcast([P, J, TW]),
               ALU.mult).then_inc(codes_ready, 1)

            def shared_sum(g):
                for t in range(g * GT, (g + 1) * GT):
                    dve.wait_ge(down_done, t + 1)
                    tt(x_early[:, t, :], x_early[:, t, :], psum[:, 4 + t % GT, :], ALU.add).then_inc(z_ready, 1)

            shared_sum(0)
            shared_hidden(1)
            dve.wait_ge(dispatch_done, 1)
            link(V.tensor_scalar(code_f[:, :], psum[:, 0, 0:TW], -float(P), float(ASSIGN), ALU.mult, ALU.add))
            link(tt(code_f[:, :], code_f[:, :], psum[:, 0, TW:2 * TW], ALU.add))
            link(V.tensor_copy(to_row[:, :], code_f[:, :]))
            V.tensor_scalar(from_row[:, 0:TW], to_row[:, :], TOKENS - 1, None, ALU.bitwise_and).then_inc(tables_ready, 1)
            shared_sum(1)

            def rows_transposed(b, done):
                dve.wait_ge(xgT_done, done)
                V.tensor_copy(xgT[:, b], psum[:, b, :].rearrange("p (c n) -> p c n", c=C)).then_inc(xgT_ready, 1)

            def hidden(i, b):
                e = dve.value_load(tile_expert[0:1, bass.ds(i, 1)], min_val=0, max_val=E - 1)
                dve.wait_ge(h_done, i + 1)
                tt(h_sb[:, b], psum[:, 2 + b, 0:2 * INTER].rearrange("p (w n) -> p w n", w=2),
                   ebias[:, bass.ds(e, 1), :, :].rearrange("p u w n -> p (u w) n"), ALU.add).then_inc(h_ready, 1)
                dve.wait_ge(s_ready, i + 1)
                tt(g_sb[:, b, :], s_sb[:, b, :], h_sb[:, b, 1, :], ALU.mult).then_inc(g_ready, 1)

            def dve_pair(p):
                rows_transposed(0, p * 2 + 1)
                rows_transposed(1, p * 2 + 2)
                hidden(p * 2, 0)
                hidden(p * 2 + 1, 1)

            dve.wait_ge(experts_loaded, 16 * EXPERT_LOADS)
            dve.wait_ge(tables_ready, 1)
            with dve.Fori(0, SURE) as p:
                dve_pair(p)
            pairs = dve.value_load(tile_counts[0:1, 0:1], min_val=SURE, max_val=PAIRS)
            with dve.Fori(SURE, PAIRS) as p:
                with dve.If(pairs > p):
                    dve_pair(p)

            def add_rows(g):
                dve.wait_ge(rows_loaded[g], 32)
                if g < EARLY:
                    dve.wait_ge(z_ready, (g + 1) * GT)
                else:
                    dve.wait_ge(x_again_loaded, 16)
                for t in range(g * GT, (g + 1) * GT):
                    acc = x_early[:, t, :] if g < EARLY else x_again[:, t - EARLY * GT, :]
                    for k in range(TOPK):
                        ins = V.scalar_tensor_tensor(out=acc, in0=rows_k[:, g % 2, k, t % GT, :],
                                                     scalar=tops[:, k, t:t + 1], in1=acc,
                                                     op0=ALU.mult, op1=ALU.add)
                        if k == 0:
                            link(ins)
                    if g < EARLY:
                        ins.then_inc(out_ready, 1)
                    else:
                        link(ins)

            def late_sum(g):
                for t in range(g * GT, (g + 1) * GT):
                    dve.wait_ge(down_done, t + 1)
                    acc = x_again[:, t - EARLY * GT, :]
                    tt(acc, acc, psum[:, 4 + t % GT, :], ALU.add).then_inc(z_ready, 1)

            shared_hidden(2)
            add_rows(0)
            add_rows(1)
            add_rows(2)
            late_sum(2)
            shared_hidden(3)
            add_rows(3)
            late_sum(3)


def kernel(**inputs):
    import numpy as np
    import concourse.bacc as bacc
    from concourse.bass_utils import run_bass_kernel_spmd

    nc = bacc.Bacc("TRN2", target_bir_lowering=False, num_devices=1)
    a = {n.removeprefix("L0_").removeprefix("cond_"): np.asarray(v) for n, v in inputs.items()}
    cond, b2 = np.asarray(inputs["cond_128"]), a["b2"]
    kernels, out_c, in_c, _ = a["weight"].shape
    chunks, dim = a["ffn_router_w"].shape[0] // P, a["ffn_router_w"].shape[0]
    experts = a["ffn_ew1"].shape[0]

    def rows(w):
        return w.reshape(-1, P, w.shape[-1]).transpose(1, 0, 2).reshape(P, -1)

    def everywhere(v):
        return np.broadcast_to(v, (P, v.size))

    mix = np.concatenate([a["weight"][..., 0].transpose(0, 2, 1), a["bias_k"][:, :, None]], axis=2)
    arrays = {
        "x": a["x"],
        "cond_pack": np.concatenate([cond.T, a["W0"], a["W1"], a["W2"], a["b0"][:, None], a["b1"][:, None],
                                     everywhere(b2), rows(mix.reshape(kernels * in_c, out_c + 1))], axis=1),
        "router_pack": np.concatenate([rows(a["ffn_router_w"]), everywhere(a["ffn_router_b"]),
                                       everywhere(a["ffn_router_bias"]), rows(a["ffn_sb1"][:, None]),
                                       rows(a["ffn_sb2"][:, None])], axis=1),
        "shared_pack": np.concatenate([rows(a["ffn_sw1"]), rows(a["ffn_sw2"]), rows(a["ffn_sw3"])], axis=1),
        "expert_pack": np.concatenate(
            [a[w].reshape(experts, -1, P, a[w].shape[2]).transpose(0, 2, 1, 3).reshape(experts, P, -1)
             for w in ("ffn_ew1", "ffn_ew2", "ffn_ew3")], axis=2),
        "expert_bias": np.concatenate([a["ffn_eb1"], a["ffn_eb2"]], axis=1).reshape(1, -1),
        "down_bias": np.concatenate([a["ffn_eb3"], a["ffn_sb3"][None, :]], axis=0),
    }
    arrays = {n: np.ascontiguousarray(v) for n, v in arrays.items()}
    args = [nc.dram_tensor(n, v.shape, mybir.dt.from_np(v.dtype), kind="ExternalInput").ap()
            for n, v in arrays.items()]
    shape = inputs['x'].shape
    args.append(nc.dram_tensor("out_dram", shape, F32, kind="ExternalOutput").ap())
    adaln_moe_ffn(nc, *args)
    r = run_bass_kernel_spmd(nc, [arrays], core_ids=[0])
    return r.results[0]["out_dram"]
```

```python
from contextlib import ExitStack

import concourse.bass as bass
from concourse import mybir

P = 128
ALU = mybir.AluOpType
ACT = mybir.ActivationFunctionType
AX_X = mybir.AxisListType.X
F32 = mybir.dt.float32
BF16 = mybir.dt.bfloat16
F32R = mybir.dt.float32r
I32 = mybir.dt.int32
U32 = mybir.dt.uint32

MASKED = -1.0e30
TAKEN = -3.0e30


def adaln_moe_ffn(nc, x, cond_pack, router_pack, shared_pack, expert_pack, expert_bias, down_bias, out):
    BS, IN_C, DIM = x.shape
    E, _, EW = expert_pack.shape
    EMB = HID = P
    KMIX = 8
    INTER = EW // (2 * DIM // P + DIM // P)
    SHARED = 2 * INTER
    TOKENS = BS * IN_C
    TOPK = 2
    NGROUPS, GSIZE = 4, E // 4
    NT = TOKENS // P
    C = DIM // P
    BPT = P // IN_C
    GT = 4
    NG = NT // GT
    EARLY = NG // 2
    LAST = NG - 1
    GN = GT * P
    IB = SHARED // P
    PARTS = 6
    GROWS = PARTS * (E + 1)
    ASSIGN = TOKENS * TOPK
    TILES = (ASSIGN + E * (P - 1)) // P
    TW = TILES + 1
    PAIRS = TW // 2
    SURE = ASSIGN // P // 2
    RING = 4

    x_rows = x.rearrange("b c d -> (b c) d")
    out_rows = out.rearrange("b c d -> (b c) d")
    xt_dram = nc.dram_tensor("xt_rows", [TOKENS, DIM], F32, kind="Internal").ap()
    y_dram = nc.dram_tensor("expert_rows", [ASSIGN, DIM], F32, kind="Internal").ap()

    ctx = ExitStack()
    with ctx:
        def sb(name, shape, dt=F32):
            return ctx.enter_context(nc.sbuf_tensor(name, shape, dt))

        def sem(name):
            return ctx.enter_context(nc.semaphore(name))

        with nc.sbuf_tensor("x_split", [P, EARLY, 2, C, GN], F32R) as x_split_sb, \
                nc.sbuf_tensor("w_split", [P, 2, 2 * C * SHARED], F32R) as w_split_sb:
            x_split, w_split = x_split_sb[:, :, :, :, :], w_split_sb[:, :, :]
        PRODUCTS = ((0, 0), (0, 1), (1, 0))
        w12_split = w_split.rearrange("p s (w c n) -> p s w c n", w=2, c=C)
        HALF = E // 2

        wexp = sb("wexp", [P, E, EW])
        ebias = sb("ebias", [P, E, 2, INTER])
        shared_sb = sb("shared_sb", [P, 2 * C * SHARED + IB * DIM])
        sw12 = shared_sb[:, 0:2 * C * SHARED].rearrange("p (w c n) -> p w c n", w=2, c=C)
        sw3_sb = shared_sb[:, 2 * C * SHARED:].rearrange("p (i n) -> p i n", i=IB)
        x_early = sb("x_early", [P, EARLY * GT, DIM])
        late_region = sb("late_region", [P, 16384 // 4])
        xT = sb("xT", [P, NG, C, GN])
        r1 = sb("r1", [P, 8192 // 4])
        xt_sb = sb("xt_sb", [P, 8192 // 4])

        x_late = late_region[:, :].rearrange("p (t d) -> p t d", d=DIM)
        onehot_slot = late_region[:, 0:2048].bitcast(BF16).rearrange("p (j s) -> p j s", s=P)
        temps = late_region[:, 2048:4096].rearrange("p (n f) -> p n f", f=NT * E)
        S, mk, cc, oh1, oh2, t5 = (temps[:, n, :] for n in range(6))
        last_temps = late_region[:, 2048 + 6 * NT * E:4096]
        gate17 = last_temps[:, 0:NT * (E + 1)].rearrange("p (t e) -> p t e", e=E + 1)
        chosen = last_temps[:, 272:272 + 128].bitcast(BF16)
        pos = last_temps[:, 400:432].rearrange("p (k t) -> p k t", k=TOPK)
        pos_i = last_temps[:, 432:464].bitcast(I32).rearrange("p (k t) -> p k t", k=TOPK)
        ptile = last_temps[:, 464:496].rearrange("p (k t) -> p k t", k=TOPK)
        xg = late_region[:, 0:2048].rearrange("p (r d) -> p r d", d=DIM)
        y_sb = late_region[:, 2048:4096].rearrange("p (r d) -> p r d", d=DIM)

        mixT = r1[:, :].rearrange("p (t m) -> p t m", m=P)
        tile_code = r1[:, 0:1536].bitcast(BF16).rearrange("p (j v t) -> p j v t", v=2, t=TW)
        xgT = r1[:, 0:1024].rearrange("p (r c n) -> p r c n", r=2, c=C)
        h_sb = r1[:, 1024:1536].rearrange("p (r w n) -> p r w n", r=2, w=2)
        s_sb = r1[:, 1536:1792].rearrange("p (r n) -> p r n", r=2)
        g_sb = r1[:, 1792:2048].rearrange("p (r n) -> p r n", r=2)

        xt_ring = xt_sb[:, :].rearrange("p (r d) -> p r d", d=DIM)
        gs_first = xt_sb[:, 0:1024].rearrange("p (i n) -> p i n", i=IB)
        gs_second = xT[:, 1, 0:IB, :]
        gs_last = late_region[:, 0:1024].rearrange("p (i n) -> p i n", i=IB)
        eb3x = xt_sb[0:GROWS, 1024:1280].bitcast(BF16)
        gT_sb = xt_sb[:, 1536:1792].rearrange("p (r n) -> p r n", r=2)

        slot_iota = xt_sb[:, 1792:1792 + P // 2].bitcast(BF16)

        cpool = xT[:, NG - 1, :, :].rearrange("p c n -> p (c n)")
        cpos = [0]

        def early(rows, cols):
            a = cpool[0:rows, cpos[0]:cpos[0] + cols]
            cpos[0] += cols
            return a

        condT, W0_sb, W1_sb, W2_sb = early(P, BS), early(P, HID), early(P, HID), early(P, KMIX)
        b0_sb, b1_sb, b2_sb = early(P, 1), early(P, 1), early(BS, KMIX)
        mix_w = early(P, KMIX * (IN_C + 1)).rearrange("p (k o) -> p k o", k=KMIX)
        cond_in = cpool[:, 0:cpos[0]]
        h1T, h2T = early(P, BS), early(P, BS)
        att, att_e = early(BS, KMIX), early(BS, KMIX)
        att_max, att_sum, att_rec = early(BS, 1), early(BS, 1), early(BS, 1)
        att_spread = early(BS, NT * KMIX).rearrange("b (t k) -> b t k", k=KMIX)
        is_tile = early(BS, NT)
        is_block = early(BS, P).rearrange("b (r i) -> b r i", r=BPT)
        mix_terms = early(P, 2 * KMIX * (IN_C + 1)).rearrange("p (t k o) -> p t k o", t=2, k=KMIX)
        mix_sum = early(P, 2 * (IN_C + 1)).rearrange("p (t o) -> p t o", t=2)
        gateT = xT[0:GROWS, 0, :, :].rearrange("p c n -> p (c n)")[:, 0:TOKENS // 2].bitcast(BF16)
        gate_parts = late_region[:, 0:NT * GROWS // 2].bitcast(BF16).rearrange("p (t j e) -> p t j e",
                                                                              j=PARTS, e=E + 1)
        gate_rest = late_region[:, 1024:1024 + NT * (E + 1)].rearrange("p (t e) -> p t e", e=E + 1)
        ident_bf = r1[:, 1536:1600].bitcast(BF16)
        small = r1[:, 1600:1600 + 3 * NT].rearrange("p (q t) -> p q t", q=3)
        ebias_flat = ebias[:, :, :, :].rearrange("p e w n -> p (e w n)")
        b3_sum, b3_rest = (ebias_flat[0:GROWS, q * DIM:(q + 1) * DIM] for q in range(2))
        b3_part, b3_kept = (ebias_flat[0:GROWS, (4 + q) * DIM // 2:(5 + q) * DIM // 2].bitcast(BF16)
                            for q in range(2))

        wexp_flat = wexp[:, :, :].rearrange("p e n -> p (e n)")
        rows_k = wexp_flat[:, 0:NG * TOPK * GT * DIM].rearrange("p (g k t d) -> p g k t d", g=NG, k=TOPK, t=GT)
        spare = xT[:, 0, :, :].rearrange("p c n -> p (c n)")[:, TOKENS // 2:]
        x_again = ([xT[:, 1, u, :] for u in range(GT)] + [xt_sb[:, u * DIM:(u + 1) * DIM] for u in range(2)]
                   + [spare[:, u * DIM:(u + 1) * DIM] for u in range(2)])
        gs_third = wexp_flat[:, NG * TOPK * GT * DIM:NG * TOPK * GT * DIM + IB * GN].rearrange(
            "p (i n) -> p i n", i=IB)

        ident = sb("ident", [P, P])
        before = sb("before", [P, P], BF16)
        ones_bf = sb("ones_bf", [P, P], BF16)
        router_sb = sb("router_sb", [P, C * E + 2 * E + 2 * IB])
        rw_sb = router_sb[:, 0:C * E].rearrange("p (c e) -> p c e", c=C)
        rb_sb = router_sb[:, C * E:C * E + E]
        rbias_sb = router_sb[:, C * E + E:C * E + 2 * E]
        sb12_sb = router_sb[:, C * E + 2 * E:].rearrange("p (w i) -> p w i", w=2)
        mix_bias = sb("mix_bias", [P, NT])
        rev_e = sb("rev_e", [P, E])
        tile_iota = sb("tile_iota", [P, TW])
        part_iota = sb("part_iota", [P, 1])
        hi_code = sb("hi_code", [P, TOPK * NT])
        lower = sb("lower", [P, NGROUPS, NGROUPS])
        restart = sb("restart", [P, NT])
        steps128 = sb("steps128", [P, NT])
        tops = sb("tops", [P, TOPK, NT])
        count = sb("count", [P, 4, E])
        pslot = sb("pslot", [P, TOPK, NT])
        tile_expert = sb("tile_expert", [P, TW], I32)
        tile_counts = sb("tile_counts", [P, 3 + RING], I32)
        N_PAIRS, N_TILES, N_TILES_LESS_2, N_SCATTERED = range(4)
        round_up = sb("round_up", [P, RING])
        last_slot = sb("last_slot", [P, RING])
        code_f = sb("code_f", [P, TW])
        to_row = sb("to_row", [P, TW], I32)
        from_row = sb("from_row", [P, TW + 2 * RING], I32)
        to_slot = sb("to_slot", [P, RING], I32)
        from_slot = sb("from_slot", [P, RING], I32)

        psum = ctx.enter_context(nc.psum_tensor("psum", [P, 8, 512], F32))

        cond_loaded = sem("cond_loaded")
        x_loaded = [sem(f"x_loaded{g}") for g in range(NG)]
        router_loaded = sem("router_loaded")
        shared_loaded = sem("shared_loaded")
        half_loaded = [sem(f"half_loaded{h}") for h in range(2)]
        part_ready = sem("part_ready")
        split_ready = sem("split_ready")
        b3_loaded = sem("b3_loaded")
        b3_ready = sem("b3_ready")
        consts_ready = sem("consts_ready")
        ident_ready = sem("ident_ready")
        masks_ready = sem("masks_ready")
        blocks_zeroed = sem("blocks_zeroed")
        ident_bf_ready = sem("ident_bf_ready")
        slots_ready = sem("slots_ready")
        pool_chain = sem("pool_chain")
        dve_chain = sem("dve_chain")
        act_chain = sem("act_chain")
        pe_cond = sem("pe_cond")
        dve_cond = sem("dve_cond")
        act_cond = sem("act_cond")
        mix_copied = sem("mix_copied")
        xt_done = sem("xt_done")
        xt_ready = sem("xt_ready")
        xt_stored = [sem(f"xt_stored{r}") for r in range(RING)]
        xtT_done = sem("xtT_done")
        xT_ready = sem("xT_ready")
        logits_done = sem("logits_done")
        shifted_ready = sem("shifted_ready")
        exp_ready = sem("exp_ready")
        gates_ready = sem("gates_ready")
        gate_part_ready = sem("gate_part_ready")
        gate_rest_ready = sem("gate_rest_ready")
        gate_parts_ready = sem("gate_parts_ready")
        gateT_done = sem("gateT_done")
        gateT_ready = sem("gateT_ready")
        chosen_ready = sem("chosen_ready")
        ranks_done = sem("ranks_done")
        ranks_read = sem("ranks_read")
        pslot_ready = sem("pslot_ready")
        squares_ready = sem("squares_ready")
        act_onehots = sem("act_onehots")
        code_base_ready = sem("code_base_ready")
        pool_codes = sem("pool_codes")
        codes_ready = sem("codes_ready")
        dispatch_done = sem("dispatch_done")
        tables_ready = sem("tables_ready")
        counts_ready = sem("counts_ready")
        up_done = sem("up_done")
        up_silu = sem("up_silu")
        up_ready = sem("up_ready")
        down_done = sem("down_done")
        z_ready = sem("z_ready")
        from_copied = sem("from_copied")
        to_copied = sem("to_copied")
        pool_held = sem("pool_held")
        xg_loaded = [sem(f"xg_loaded{r}") for r in range(RING)]
        xgT_done = sem("xgT_done")
        xgT_ready = sem("xgT_ready")
        h_done = sem("h_done")
        h_ready = sem("h_ready")
        s_ready = sem("s_ready")
        g_ready = sem("g_ready")
        gT_done = sem("gT_done")
        gT_ready = sem("gT_ready")
        y_done = sem("y_done")
        y_ready = sem("y_ready")
        scattered = [sem(f"scattered{r}") for r in range(RING)]
        x_again_loaded = sem("x_again_loaded")
        rows_loaded = [sem(f"rows_loaded{g}") for g in range(NG)]
        last_scaled = sem("last_scaled")
        last_added = sem("last_added")
        out_ready = sem("out_ready")
        out_stored = sem("out_stored")

        GATE_BANKS = (4, 2, 3, 5)
        UP_BANKS = (0, 2, 6, 0, 0, 2, 0, 2)
        DOWN_BANKS = (4, 5, 6, 7, 2, 3, 4, 5) + (4, 5, 6, 7) * (NG - EARLY)
        J_ACT = 8
        J_DVE = 22
        SPLITS = EARLY * GT + 4
        MIXES = [(0, 1), (1, 2)] + [(t, t + 2) for t in range(2, NT, 2)]

        block = ctx.enter_context(nc.Block())

        def x_tile(t):
            return x_early[:, t, :] if t < EARLY * GT else x_late[:, t - EARLY * GT, :]

        def gs_of(g):
            return (gs_first, gs_second, gs_third, gs_last)[g]

        def split_of(u):
            if u < EARLY * GT:
                g, cols = u // GT, slice((u % GT) * P, (u % GT + 1) * P)
                return xT[:, g, :, cols], x_split[:, g, 0, :, cols], x_split[:, g, 1, :, cols]
            n = 2 * C * SHARED // 4
            cols = slice((u - EARLY * GT) * n, (u - EARLY * GT + 1) * n)
            return shared_sb[:, cols], w_split[:, 0, cols], w_split[:, 1, cols]

        def mixes_until(t):
            return next(n + 1 for n, (first, end) in enumerate(MIXES) if first <= t < end)

        def group_of_x(g):
            return x_rows[g * GN:(g + 1) * GN, :].rearrange("(t p) d -> p t d", p=P)

        def acc_tile(t):
            g = t // GT
            return x_early[:, t, :] if g < EARLY else x_again[t - EARLY * GT]

        def xT_tile(t, c):
            return xT[:, t // GT, c, (t % GT) * P:(t % GT + 1) * P]

        def count_of(engine, n):
            extra = (0, 16, 0, -16)
            low, high = {N_PAIRS: (SURE, PAIRS), N_TILES: (2 * SURE, 2 * PAIRS),
                         N_TILES_LESS_2: (2 * SURE - 2, 2 * PAIRS - 2),
                         **{N_SCATTERED + r: (8 * SURE + extra[r], 8 * PAIRS + extra[r]) for r in range(RING)}}[n]
            return engine.value_load(tile_counts[0:1, n:n + 1], min_val=low, max_val=high)

        def store_group(sp, g):
            for t in range(g * GT, (g + 1) * GT):
                sp.wait_ge(*((out_ready, t + 1) if g < EARLY else (z_ready, t + 1)))
                sp.dma_start(out_rows[t * P:(t + 1) * P, :], acc_tile(t)).then_inc(out_stored, 16)

        @block.sync
        def _(sp):
            sp.dma_start(cond_in, cond_pack).then_inc(cond_loaded, 16)
            for g in range(NG):
                dst = x_early[:, g * GT:(g + 1) * GT, :] if g < EARLY else \
                    x_late[:, (g - EARLY) * GT:(g - EARLY + 1) * GT, :]
                sp.dma_start(dst, group_of_x(g)).then_inc(x_loaded[g], 16)
                if g == 0:
                    sp.dma_start(router_sb[:, :], router_pack).then_inc(router_loaded, 16)
                    sp.dma_start(b3_sum, down_bias).then_inc(b3_loaded, 16)
            sp.dma_start(shared_sb[:, :], shared_pack).then_inc(shared_loaded, 16)
            for t in range(NT):
                sp.wait_ge(xt_ready, t + 1)
                sp.dma_start(xt_dram[t * P:(t + 1) * P, :], xt_ring[:, t % RING, :]
                             ).then_inc(xt_stored[t % RING], 16)
                if t % 2 == 1:
                    place = HALF + t // 2
                    sp.dma_start(wexp[:, place, :], expert_pack[place]).then_inc(half_loaded[0], 16)
            sp.wait_ge(b3_ready, 1)
            sp.dma_start(ebias_flat, expert_bias.to_broadcast([P, E * 2 * INTER])).then_inc(half_loaded[0], 16)
            FIRST_PLACES = 2 * C * GN // EW
            for place in range(HALF):
                if place == 0:
                    sp.wait_ge(up_done, IB)
                if place == FIRST_PLACES:
                    sp.wait_ge(up_done, EARLY * IB)
                sp.dma_start(wexp[:, place, :], expert_pack[place]).then_inc(half_loaded[1], 16)
            sp.wait_ge(down_done, EARLY * GT)
            for t in range(EARLY * GT, NT):
                sp.dma_start(acc_tile(t), x_rows[t * P:(t + 1) * P, :]).then_inc(x_again_loaded, 16)
            sp.wait_ge(counts_ready, 1)
            tiles = count_of(sp, N_TILES)
            all_scattered = [count_of(sp, N_SCATTERED + r) for r in range(RING)]
            sp.wait_ge(y_done, tiles)
            for r in range(RING):
                sp.wait_ge(scattered[r], all_scattered[r])
            for g in range(NG):
                for k in range(TOPK):
                    src = y_dram[k * TOKENS + g * GN:k * TOKENS + (g + 1) * GN, :]
                    sp.dma_start(rows_k[:, g, k], src.rearrange("(t p) d -> p t d", p=P)
                                 ).then_inc(rows_loaded[g], 16)
            for g in range(NG):
                store_group(sp, g)
            sp.wait_ge(out_stored, 16 * NT)

        @block.gpsimd
        def _(pool):
            n = [0]

            def link(ins):
                n[0] += 1
                ins.then_inc(pool_chain, 1)
                pool.wait_ge(pool_chain, n[0])

            link(nc.gpsimd.memset(ident[:, :], 0.0))
            nc.gpsimd.affine_select(out=ident[:, :], in_=ident[:, :], compare_op=ALU.not_equal, fill=1.0,
                                    base=0, pattern=[[-1, P]], channel_multiplier=1).then_inc(ident_ready, 1)
            link(nc.gpsimd.memset(is_tile, 0.0))
            for r in range(BPT):
                link(nc.gpsimd.affine_select(out=is_tile, in_=is_tile, compare_op=ALU.not_equal, fill=1.0,
                                             base=-NT * r, pattern=[[-1, NT]], channel_multiplier=1))
            link(nc.gpsimd.memset(is_block, 1.0))
            link(nc.gpsimd.affine_select(out=is_block, in_=is_block, compare_op=ALU.is_ge, fill=0.0, base=0,
                                         pattern=[[-NT, BPT], [0, IN_C]], channel_multiplier=1))
            nc.gpsimd.affine_select(out=is_block, in_=is_block, compare_op=ALU.is_ge, fill=0.0, base=NT - 1,
                                    pattern=[[NT, BPT], [0, IN_C]], channel_multiplier=-1
                                    ).then_inc(masks_ready, 1)
            nc.gpsimd.memset(r1[:, :], 0.0).then_inc(blocks_zeroed, 1)
            link(nc.gpsimd.memset(ones_bf[:, :], 1.0))
            link(nc.gpsimd.affine_select(out=before[:, :], in_=ones_bf[:, :], compare_op=ALU.is_gt, fill=0.0,
                                         base=0, pattern=[[1, P]], channel_multiplier=-1))
            for dst, pattern, base, mult in (
                    (rev_e[:, :], [[-1, E]], E, 0),
                    (tile_iota[:, :], [[1, TW]], 0, 0), (part_iota[:, :], [[1, 1]], 0, 1),
                    (hi_code[:, :], [[-1, TOPK * NT]], TOPK * NT, 0),
                    (restart[:, :], [[1, NT]], 0, 0), (steps128[:, :], [[P, NT]], 0, 0),
                    (lower[:, :, :], [[1, NGROUPS], [-1, NGROUPS]], 0, 0)):
                link(nc.gpsimd.iota(dst, pattern=pattern, base=base, channel_multiplier=mult,
                                    allow_small_or_imprecise_dtypes=True))
            link(nc.gpsimd.tensor_scalar(restart[:, :], restart[:, :], 1.0, None, ALU.min))
            link(nc.gpsimd.tensor_scalar(lower[:, :, :], lower[:, :, :], 0.0, None, ALU.is_gt))
            link(nc.gpsimd.memset(round_up[:, :], 1.0))
            nc.gpsimd.memset(round_up[:, 1:3], 0.0)
            link(nc.gpsimd.memset(last_slot[:, :], 0.0))
            nc.gpsimd.memset(last_slot[:, 1:2], 16.0)
            nc.gpsimd.memset(last_slot[:, 3:4], -16.0)
            nc.gpsimd.memset(from_row[:, TW:], 0).then_inc(consts_ready, 1)

            pool.wait_ge(b3_loaded, 16)
            T = nc.gpsimd

            def keep_rows(dst, src, first, end):
                if first > 0:
                    link(T.affine_select(out=dst, in_=src, compare_op=ALU.is_ge, fill=0.0, base=-first,
                                         pattern=[[0, DIM]], channel_multiplier=1))
                    src = dst
                if end < GROWS:
                    link(T.affine_select(out=dst, in_=src, compare_op=ALU.is_ge, fill=0.0, base=end - 1,
                                         pattern=[[0, DIM]], channel_multiplier=-1))

            link(T.tensor_copy(b3_part, b3_sum))
            link(T.tensor_tensor(b3_rest, b3_sum, b3_part, ALU.subtract))
            keep_rows(b3_sum, b3_part, 0, 3 * (E + 1))
            link(T.tensor_copy(b3_part, b3_rest))
            link(T.tensor_tensor(b3_rest, b3_rest, b3_part, ALU.subtract))
            keep_rows(b3_kept, b3_part, 3 * (E + 1), 5 * (E + 1))
            link(T.tensor_tensor(b3_sum, b3_sum, b3_kept, ALU.add))
            keep_rows(b3_rest, b3_rest, 5 * (E + 1), GROWS)
            link(T.tensor_tensor(b3_sum, b3_sum, b3_rest, ALU.add))
            for u in range(SPLITS):
                pool.wait_ge(part_ready, u + 1)
                whole, part, rest = split_of(u)
                T.tensor_tensor(rest, whole, part, ALU.subtract).then_inc(split_ready, 1)
            pool.wait_ge(xtT_done, NT)
            for r in range(RING):
                pool.wait_ge(xt_stored[r], 16 * (NT // RING))
            T.tensor_copy(eb3x, b3_sum).then_inc(b3_ready, 1)
            T.tensor_copy(ident_bf, ident[:, :]).then_inc(ident_bf_ready, 1)
            nc.gpsimd.iota(slot_iota, pattern=[[1, P]], base=0, channel_multiplier=0,
                           allow_small_or_imprecise_dtypes=True).then_inc(slots_ready, 1)
            pool.wait_ge(gate_part_ready, 1)
            T.tensor_tensor(gate_rest, gate17, gate_parts[:, :, 0], ALU.subtract).then_inc(gate_rest_ready, 1)
            pool.wait_ge(gate_part_ready, 2)
            pool.wait_ge(gate_rest_ready, 1)
            T.tensor_tensor(gate_rest, gate_rest, gate_parts[:, :, 1], ALU.subtract).then_inc(gate_rest_ready, 1)
            pool.wait_ge(code_base_ready, 1)
            T.tensor_tensor(tile_code[:, J_DVE:, 0, :], tile_code[:, J_DVE:, 0, :],
                            hi_code[:, J_DVE:].unsqueeze(2).to_broadcast([P, TOPK * NT - J_DVE, TW]), ALU.mult
                            ).then_inc(pool_codes, 1)
            pool.wait_ge(tables_ready, 1)

            def hold(semaphore, value):
                pool.wait_ge(semaphore, value)
                pool.sem_inc(pool_held, 1)

            def gather(i, slot):
                nc.gpsimd.tensor_copy(from_slot[:, slot:slot + 1], from_row[:, bass.ds(i, 1)]
                                      ).then_inc(from_copied, 1)
                hold(from_copied, i + 1)
                nc.gpsimd.indirect_dma_start(
                    out=xg[:, slot, :], out_offset=None, in_=xt_dram[:, :],
                    in_offset=bass.IndirectOffsetOnAxis(ap=from_slot[:, slot:slot + 1].bitcast(U32), axis=0),
                ).then_inc(xg_loaded[slot], 16)

            def scatter(i, slot):
                hold(y_ready, i + 1)
                nc.gpsimd.tensor_copy(to_slot[:, slot:slot + 1], to_row[:, bass.ds(i, 1)]
                                      ).then_inc(to_copied, 1)
                hold(to_copied, i + 1)
                nc.gpsimd.indirect_dma_start(
                    out=y_dram[:, :],
                    out_offset=bass.IndirectOffsetOnAxis(ap=to_slot[:, slot:slot + 1].bitcast(U32), axis=0),
                    in_=y_sb[:, slot, :], in_offset=None, bounds_check=ASSIGN - 1, oob_is_err=False,
                ).then_inc(scattered[slot], 16)

            def gather_ahead(i, u):
                hold(xgT_done, i + 3)
                gather(i + 6, (u + 2) % RING)

            def pool_step(i, u):
                gather_ahead(i, u)
                scatter(i - 1, (u - 1) % RING)

            def pool_pair(p, q):
                for u in range(2):
                    pool_step(p * 2 + u, 2 * q + u)

            for i in range(RING):
                gather(i, i)
            pool.wait_ge(counts_ready, 1)
            pairs, tiles = count_of(pool, N_PAIRS), count_of(pool, N_TILES)
            gather_ahead(-2, -2)
            gather_ahead(-1, -1)
            gather_ahead(0, 0)
            pool_step(1, 1)
            pool_pair(1, 1)
            with pool.Fori(1, (SURE - 2) // 2) as j:
                for q in range(2):
                    pool_pair(j * 2 + q, q)
            def closing_pair(p, q):
                with pool.If(pairs > p + 2):
                    pool_pair(p, q)
                with pool.If(pairs < p + 3):
                    for u in range(2):
                        scatter(p * 2 + u - 1, (2 * q + u - 1) % RING)

            for q in range(2):
                closing_pair(SURE - 2 + q, q)
            for q in range(2):
                with pool.If(pairs > SURE + q):
                    closing_pair(SURE + q, q)
            with pool.If(pairs > SURE + 2):
                with pool.Fori(1, (PAIRS - SURE) // 2) as j:
                    for q in range(2):
                        p = j * 2 + SURE + q
                        with pool.If(pairs > p):
                            closing_pair(p, q)
            scatter(tiles - 1, 1)
            pool.wait_ge(x_again_loaded, 16 * (NT - EARLY * GT))
            for u in range(GT):
                t = LAST * GT + u
                pool.wait_ge(last_scaled, u + 1)
                nc.gpsimd.tensor_tensor(acc_tile(t), acc_tile(t), rows_k[:, LAST, 1, u, :], op=ALU.add
                                        ).then_inc(last_added, 1)

        @block.tensor
        def _(pe):
            def mm(dst, lhsT, rhs, start=True, stop=True):
                return nc.tensor.matmul(dst, lhsT, rhs, start=start, stop=stop)

            def keep_warm(products):
                for _ in range(products):
                    mm(psum[:, 7, 0:P], ident[:, :], ident[:, :])

            pe.wait_ge(ident_ready, 1)
            keep_warm(4)
            pe.wait_ge(cond_loaded, 16)
            mm(psum[:, 2, 0:BS], W0_sb, condT).then_inc(pe_cond, 1)
            keep_warm(4)
            pe.wait_ge(act_cond, 1)
            mm(psum[:, 3, 0:BS], W1_sb, h1T).then_inc(pe_cond, 1)
            keep_warm(2)
            pe.wait_ge(act_cond, 2)
            mm(psum[0:BS, 4, 0:KMIX], h2T, W2_sb).then_inc(pe_cond, 1)
            keep_warm(8)
            pe.wait_ge(masks_ready, 1)
            pe.wait_ge(dve_cond, 2)
            mm(psum[:, 5, 0:NT * KMIX], is_block.rearrange("b r i -> b (r i)"),
               att_spread.rearrange("b t k -> b (t k)")).then_inc(pe_cond, 1)
            keep_warm(8)

            for s in range(NT + 2):
                if s < NT:
                    if s % GT == 0:
                        pe.wait_ge(x_loaded[s // GT], 16)
                    pe.wait_ge(mix_copied, mixes_until(s))
                    if s >= 2:
                        pe.wait_ge(xt_ready, s - 1)
                    mm(psum[:, s % 2, :], mixT[:, s, :], x_tile(s)).then_inc(xt_done, 1)
                if 1 <= s <= NT:
                    t = s - 1
                    if t == 0:
                        pe.wait_ge(ident_ready, 1)
                    pe.wait_ge(xt_ready, t + 1)
                    if t >= 2:
                        pe.wait_ge(xT_ready, t - 1)
                    for c in range(C):
                        last = nc.tensor.transpose(psum[:, 2 + t % 2, c * P:(c + 1) * P],
                                                   xt_ring[:, t % RING, c * P:(c + 1) * P], ident[:, :])
                    last.then_inc(xtT_done, 1)
                if s >= 2:
                    t = s - 2
                    if t == 0:
                        pe.wait_ge(router_loaded, 16)
                    pe.wait_ge(xT_ready, t + 1)
                    for c in range(C):
                        last = mm(psum[:, 4, t * E:(t + 1) * E], xT_tile(t, c), rw_sb[:, c, :],
                                  start=(c == 0), stop=(c == C - 1))
            last.then_inc(logits_done, 1)

            def shared_up(g, i, between=()):
                between = dict(between)
                n = g * IB + i
                bank = UP_BANKS[n]
                if n >= 3:
                    pe.wait_ge(up_ready, 1 if n == 3 else n - 1)
                for w in range(2):
                    for c in range(C):
                        cols = slice(i * P, (i + 1) * P)
                        if g < EARLY:
                            for n_product, (a, b) in enumerate(PRODUCTS):
                                last = mm(psum[:, bank + w, :], w12_split[:, a, w, c, cols], x_split[:, g, b, c, :],
                                          start=(c == 0 and n_product == 0),
                                          stop=(c == C - 1 and n_product == len(PRODUCTS) - 1))
                        else:
                            last = mm(psum[:, bank + w, :], sw12[:, w, c, cols], xT[:, g, c, :],
                                      start=(c == 0), stop=(c == C - 1))
                        if (w, c) == (1, C - 1):
                            last.then_inc(up_done, 1)
                        if (w, c) in between:
                            between[w, c]()

            def shared_down(g, tiles=range(GT)):
                pe.wait_ge(up_ready, IB * (g + 1))
                for t in (g * GT + u for u in tiles):
                    if t == 0:
                        pe.wait_ge(gateT_ready, 1)
                    elif t == 1:
                        pe.wait_ge(gateT_ready, NG)
                    elif t == 2:
                        pe.wait_ge(up_ready, 3)
                    elif t in (6, 7):
                        pe.wait_ge(z_ready, t - 5)
                    elif t >= 8:
                        pe.wait_ge(z_ready, t - GT + 1)
                    bank = psum[:, DOWN_BANKS[t], :]
                    for i in range(IB):
                        mm(bank, gs_of(g)[:, i, (t % GT) * P:(t % GT + 1) * P], sw3_sb[:, i, :],
                           start=(i == 0), stop=False)
                    if t == 0:
                        pe.wait_ge(b3_ready, 1)
                    mm(bank, gateT[:, t * P:(t + 1) * P], eb3x, start=False, stop=True).then_inc(down_done, 1)

            pe.wait_ge(shared_loaded, 16)
            pe.wait_ge(split_ready, SPLITS)
            shared_up(0, 0)
            shared_up(0, 1)
            shared_up(1, 0)
            pe.wait_ge(chosen_ready, 1)
            mm(psum[:, 5, 0:NT * E], before[:, :], chosen)
            mm(psum[:, 5, NT * E:2 * NT * E], ones_bf[:, :], chosen).then_inc(ranks_done, 1)

            def gates_transposed():
                pe.wait_ge(gate_parts_ready, 1)
                pe.wait_ge(ident_bf_ready, 1)
                pe.wait_ge(up_ready, 2)
                pe.wait_ge(ranks_read, 1)
                for t in range(NT):
                    last = mm(psum[0:GROWS, GATE_BANKS[t // GT], (t % GT) * P:(t % GT + 1) * P],
                              gate_parts[:, t, :, :].rearrange("p j e -> p (j e)"), ident_bf)
                    if t % GT == GT - 1:
                        last.then_inc(gateT_done, 1)

            shared_up(1, 1)
            gates_transposed()
            shared_down(0)
            shared_down(1, [0])
            pe.wait_ge(codes_ready, 1)
            pe.wait_ge(pool_codes, 1)
            pe.wait_ge(act_onehots, 1)
            for j in range(TOPK * NT):
                last = mm(psum[:, 1, 0:2 * TW], onehot_slot[:, j, :],
                          tile_code[:, j, :, :].rearrange("p v t -> p (v t)"),
                          start=(j == 0), stop=(j == TOPK * NT - 1))
            last.then_inc(dispatch_done, 1)
            shared_down(1, range(1, GT - 1))

            pe.wait_ge(tables_ready, 1)

            def rows_transposed(b, slot, loaded):
                pe.wait_ge(xg_loaded[slot], loaded)
                for c in range(C):
                    last = nc.tensor.transpose(psum[:, b, c * P:(c + 1) * P], xg[:, slot, c * P:(c + 1) * P],
                                               ident[:, :])
                last.then_inc(xgT_done, 1)

            def up(b, e, half):
                for c in range(half * C // 2, (half + 1) * C // 2):
                    w = wexp[:, bass.ds(e, 1), 0:2 * C * INTER].rearrange("p u (w c n) -> p (u w) c n", w=2, c=C)
                    last = mm(psum[:, 2 + b, 0:2 * INTER].rearrange("p (w n) -> p w n", w=2), xgT[:, b, c, :],
                              w[:, :, c, :], start=(c == 0), stop=(c == C - 1))
                return last

            def hidden_transposed(b, ready):
                pe.wait_ge(g_ready, ready)
                nc.tensor.transpose(psum[:, 4 + b, 0:P], g_sb[:, b, :], ident[:, :]).then_inc(gT_done, 1)

            def down(b, e, ready, freed):
                pe.wait_ge(gT_ready, ready)
                if freed is not None:
                    pe.wait_ge(y_ready, freed)
                mm(psum[:, 6 + b, :], gT_sb[:, b, :],
                   wexp[:, bass.ds(e, 1), 2 * C * INTER:].rearrange("p u n -> p (u n)")).then_inc(y_done, 1)

            def expert_of(i):
                return pe.value_load(tile_expert[0:1, bass.ds(i, 1)], min_val=0, max_val=E - 1)

            def pe_step(i, b, slot, loaded):
                n = i if isinstance(i, int) else 3
                e = expert_of(i)
                pe.wait_ge(xgT_ready, i + 1)
                if n == 0:
                    pe.wait_ge(z_ready, EARLY * GT - 1)
                up(b, e, 0)
                if n == 1:
                    pe.wait_ge(z_ready, EARLY * GT)
                if n >= 1:
                    hidden_transposed(1 - b, i)
                up(b, e, 1).then_inc(h_done, 1)
                rows_transposed(b, slot, loaded)
                if n >= 1:
                    down(1 - b, expert_of(i - 1), i, i - 2 if n >= 3 else None)

            def pe_pair(p, q, loaded):
                for u in range(2):
                    pe_step(p * 2 + u, u, (2 * q + u + 2) % RING, loaded)

            rows_transposed(0, 0, 16)
            shared_down(1, [GT - 1])
            rows_transposed(1, 1, 16)
            pe.wait_ge(half_loaded[0], 16 * (HALF + 1))
            pe.wait_ge(half_loaded[1], 16 * HALF)
            pe.wait_ge(counts_ready, 1)
            pairs = count_of(pe, N_PAIRS)
            pe_pair(0, 0, 16)
            tiles = count_of(pe, N_TILES)
            pe_pair(1, 1, 32)
            tiles_less_2 = count_of(pe, N_TILES_LESS_2)
            with pe.Fori(1, SURE // 2) as j:
                pe_pair(j * 2, 0, j * 16 + 16)
                pe_pair(j * 2 + 1, 1, j * 16 + 32)
            for q in range(2):
                with pe.If(pairs > SURE + q):
                    pe_pair(SURE + q, q, 16 * (SURE // 2 + 1 + q))
            with pe.If(pairs > SURE + 2):
                with pe.Fori(1, (PAIRS - SURE) // 2) as j:
                    for q in range(2):
                        p = j * 2 + SURE + q
                        with pe.If(pairs > p):
                            pe_pair(p, q, j * 16 + 16 * (SURE // 2 + 1 + q))

            last_expert = expert_of(tiles - 1)
            pe.wait_ge(xgT_ready, tiles + 2)
            shared_up(2, 0, between={(0, 1): lambda: hidden_transposed(1, tiles),
                                     (0, 2): lambda: down(1, last_expert, tiles, tiles_less_2)})
            shared_up(2, 1)
            shared_up(3, 0)
            shared_up(3, 1)
            pe.wait_ge(y_ready, tiles)
            shared_down(2)
            shared_down(3)

        @block.scalar
        def _(act):
            act.wait_ge(ident_ready, 1)
            nc.scalar.activation(att_max, ident[0:BS, 0:1], ACT.Gelu).then_inc(act_chain, 1)
            act.wait_ge(cond_loaded, 16)
            act.wait_ge(pe_cond, 1)
            nc.scalar.activation(h1T, psum[:, 2, 0:BS], ACT.Gelu, bias=b0_sb).then_inc(act_cond, 1)
            act.wait_ge(pe_cond, 2)
            nc.scalar.activation(h2T, psum[:, 3, 0:BS], ACT.Gelu, bias=b1_sb).then_inc(act_cond, 1)
            act.wait_ge(dve_cond, 1)
            nc.scalar.activation(att_e, att, ACT.Exp, accum_out=att_sum).then_inc(act_cond, 1)
            for t in range(NT):
                act.wait_ge(mix_copied, mixes_until(t))
                act.wait_ge(xt_done, t + 1)
                if t >= RING:
                    act.wait_ge(xt_stored[t % RING], 16 * (t // RING))
                    act.wait_ge(xtT_done, t - RING + 1)
                nc.scalar.activation(xt_ring[:, t % RING, :], psum[:, t % 2, :], ACT.Identity,
                                     bias=mix_bias[:, t:t + 1]).then_inc(xt_ready, 1)
                if 2 <= t < 2 + SPLITS:
                    u = t - 2
                    if u < EARLY * GT:
                        act.wait_ge(xT_ready, u + 1)
                    else:
                        act.wait_ge(shared_loaded, 16)
                    whole, part, _ = split_of(u)
                    nc.scalar.activation(part, whole, ACT.Copy).then_inc(part_ready, 1)
            act.wait_ge(shifted_ready, 1)
            nc.scalar.activation(mk, S, ACT.Exp).then_inc(exp_ready, 1)

            def shared_silu(g, blocks=range(IB)):
                for i in blocks:
                    act.wait_ge(up_done, g * IB + i + 1)
                    nc.scalar.activation(gs_of(g)[:, i, :], psum[:, UP_BANKS[g * IB + i], :], ACT.Silu,
                                         bias=sb12_sb[:, 0, i:i + 1]).then_inc(up_silu, 1)

            act.wait_ge(router_loaded, 16)
            act.wait_ge(xtT_done, NT)
            for r in range(RING):
                act.wait_ge(xt_stored[r], 16 * (NT // RING))
            shared_silu(0)
            shared_silu(1, [0])
            act.wait_ge(gates_ready, 1)
            nc.scalar.activation(gate_parts[:, :, 0], gate17, ACT.Copy).then_inc(gate_part_ready, 1)
            act.wait_ge(gate_rest_ready, 1)
            nc.scalar.activation(gate_parts[:, :, 1], gate_rest, ACT.Copy).then_inc(gate_part_ready, 1)
            act.wait_ge(gate_part_ready, 2)
            nc.scalar.activation(gate_parts[:, :, 3:5], gate_parts[:, :, 0:2], ACT.Copy)
            nc.scalar.activation(gate_parts[:, :, 5], gate_parts[:, :, 0], ACT.Copy)
            act.wait_ge(gate_rest_ready, 2)
            nc.scalar.activation(gate_parts[:, :, 2], gate_rest, ACT.Copy).then_inc(gate_parts_ready, 1)
            for q in range(NG):
                act.wait_ge(gateT_done, q + 1)
                nc.scalar.activation(gateT[:, q * GN:(q + 1) * GN], psum[0:GROWS, GATE_BANKS[q], :], ACT.Copy
                                     ).then_inc(gateT_ready, 1)
            shared_silu(1, [1])
            act.wait_ge(pslot_ready, 1)
            act.wait_ge(gateT_done, NG)
            act.wait_ge(slots_ready, 1)
            for j in range(TOPK * NT - J_ACT, TOPK * NT):
                nc.scalar.activation(onehot_slot[:, j, :], slot_iota, ACT.Square, scale=-1.0,
                                     bias=pslot[:, j // NT, j % NT:j % NT + 1]).then_inc(squares_ready, 1)
            act.wait_ge(squares_ready, J_ACT)
            squares = onehot_slot[:, TOPK * NT - J_ACT:, :]
            nc.scalar.activation(squares, squares, ACT.Relu, scale=-1.0, bias=1.0).then_inc(act_onehots, 1)

            def hidden_transposed(b, done):
                act.wait_ge(gT_done, done)
                nc.scalar.activation(gT_sb[:, b, :], psum[:, 4 + b, 0:P], ACT.Copy).then_inc(gT_ready, 1)

            def silu(b, done):
                act.wait_ge(h_ready, done)
                nc.scalar.activation(s_sb[:, b, :], h_sb[:, b, 0, :], ACT.Silu).then_inc(s_ready, 1)

            def result(b, slot, done, freed):
                act.wait_ge(y_done, done)
                if freed is not None:
                    act.wait_ge(scattered[slot], freed)
                nc.scalar.activation(y_sb[:, slot, :], psum[:, 6 + b, :], ACT.Copy).then_inc(y_ready, 1)

            def act_step(i, b, slot, freed):
                first = isinstance(i, int) and i == 0
                if not first:
                    hidden_transposed(1 - b, i)
                silu(b, i + 1)
                if not first:
                    result(1 - b, slot, i, freed)

            def act_pair(p, q, freed):
                for u in range(2):
                    act_step(p * 2 + u, u, (2 * q + u - 1) % RING, freed[u])

            act_pair(0, 0, (None, None))
            act_pair(1, 1, (None, None))
            act_pair(2, 0, (None, 16))
            act_pair(3, 1, (16, 16))
            with act.Fori(2, SURE // 2) as j:
                act_pair(j * 2, 0, (j * 16 - 16, j * 16))
                act_pair(j * 2 + 1, 1, (j * 16, j * 16))
            act.wait_ge(counts_ready, 1)
            pairs, tiles = count_of(act, N_PAIRS), count_of(act, N_TILES)
            for q in range(2):
                turn = 16 * (SURE // 2)
                with act.If(pairs > SURE + q):
                    act_pair(SURE + q, q, (turn - 16 if q == 0 else turn, turn))
            with act.If(pairs > SURE + 2):
                with act.Fori(1, (PAIRS - SURE) // 2) as j:
                    for q in range(2):
                        p = j * 2 + SURE + q
                        turn = j * 16 + 16 * (SURE // 2)
                        with act.If(pairs > p):
                            act_pair(p, q, (turn - 16 if q == 0 else turn, turn))
            hidden_transposed(1, tiles)
            result(1, 1, tiles, count_of(act, N_SCATTERED + 2))
            shared_silu(2)
            shared_silu(3)
            act.wait_ge(rows_loaded[LAST], 16 * TOPK)
            for u in range(GT):
                rows = rows_k[:, LAST, 1, u, :]
                t = LAST * GT + u
                nc.scalar.activation(rows, rows, ACT.Copy, scale=tops[:, 1, t:t + 1]).then_inc(last_scaled, 1)

        @block.vector
        def _(dve):
            n = [0]

            def link(ins):
                n[0] += 1
                ins.then_inc(dve_chain, 1)
                dve.wait_ge(dve_chain, n[0])

            def tt(dst, a, b, op):
                return nc.vector.tensor_tensor(dst, a, b, op)

            V = nc.vector
            dve.wait_ge(pe_cond, 3)
            dve.wait_ge(cond_loaded, 16)
            link(tt(att, psum[0:BS, 4, 0:KMIX], b2_sb, ALU.add))
            dve.wait_ge(act_chain, 1)
            link(V.tensor_reduce(att_max, att, AX_X, ALU.max))
            V.tensor_scalar(att, att, att_max, None, ALU.subtract).then_inc(dve_cond, 1)
            dve.wait_ge(act_cond, 3)
            link(V.reciprocal(att_rec, att_sum))
            dve.wait_ge(masks_ready, 1)
            V.scalar_tensor_tensor(out=att_spread, in0=att_e.unsqueeze(1).to_broadcast([BS, NT, KMIX]),
                                   scalar=att_rec, in1=is_tile.unsqueeze(2).to_broadcast([BS, NT, KMIX]),
                                   op0=ALU.mult, op1=ALU.mult).then_inc(dve_cond, 1)
            dve.wait_ge(pe_cond, 4)
            dve.wait_ge(blocks_zeroed, 1)

            def mix(first, end):
                T = end - first
                att_here = psum[:, 5, first * KMIX:end * KMIX].rearrange("p (t k) -> p t k", k=KMIX)
                link(tt(mix_terms[:, 0:T], mix_w.unsqueeze(1).to_broadcast([P, T, KMIX, IN_C + 1]),
                        att_here.unsqueeze(3).to_broadcast([P, T, KMIX, IN_C + 1]), ALU.mult))
                link(V.tensor_reduce(mix_sum[:, 0:T], mix_terms[:, 0:T].rearrange("p t k o -> p t o k"),
                                     AX_X, ALU.add))
                V.tensor_copy(mix_bias[:, first:end], mix_sum[:, 0:T, IN_C])
                for b in range(BPT):
                    rows = slice(b * IN_C, (b + 1) * IN_C)
                    last = V.tensor_copy(mixT[rows, first:end, b * IN_C:(b + 1) * IN_C],
                                         mix_sum[rows, 0:T, 0:IN_C])
                last.then_inc(mix_copied, 1)

            for step in range(3):
                mix(*MIXES[step])
            for t in range(NT):
                dve.wait_ge(xtT_done, t + 1)
                if t == (NG - 1) * GT:
                    dve.wait_ge(mix_copied, len(MIXES))
                V.tensor_copy(xT[:, t // GT, :, (t % GT) * P:(t % GT + 1) * P],
                              psum[:, 2 + t % 2, :].rearrange("p (c n) -> p c n", c=C)).then_inc(xT_ready, 1)
                if t % 2 == 0 and 3 + t // 2 < len(MIXES):
                    mix(*MIXES[3 + t // 2])

            def te(a):
                return a.rearrange("p (t e) -> p t e", e=E)

            def over_e(a):
                return a.unsqueeze(2).to_broadcast([P, NT, E])

            def over_t(a):
                return a.unsqueeze(1).to_broadcast([P, NT, E])

            dve.wait_ge(logits_done, 1)
            dve.wait_ge(router_loaded, 16)
            dve.wait_ge(consts_ready, 1)
            link(tt(te(S), te(psum[:, 4, 0:NT * E]), over_t(rb_sb[:, :]), ALU.add))
            link(V.tensor_reduce(small[:, 0, :], te(S), AX_X, ALU.max))
            tt(te(S), te(S), over_e(small[:, 0, :]), ALU.subtract).then_inc(shifted_ready, 1)
            dve.wait_ge(exp_ready, 1)
            link(V.tensor_reduce(small[:, 0, :], te(mk), AX_X, ALU.add))
            link(V.reciprocal(small[:, 1, :], small[:, 0, :]))
            link(tt(te(S), te(mk), over_e(small[:, 1, :]), ALU.mult))
            link(tt(te(S), te(S), over_t(rbias_sb[:, :]), ALU.add))

            gmax = cc[:, 0:NT * NGROUPS]
            link(V.tensor_reduce(gmax, S.rearrange("p (n s) -> p n s", s=GSIZE), AX_X, ALU.max))
            gm = gmax.rearrange("p (t g) -> p t g", g=NGROUPS)
            other = gm.unsqueeze(2).to_broadcast([P, NT, NGROUPS, NGROUPS])
            own = gm.unsqueeze(3).to_broadcast([P, NT, NGROUPS, NGROUPS])

            def tgg(a):
                return a.rearrange("p (t g h) -> p t g h", g=NGROUPS, h=NGROUPS)

            tt(tgg(oh1), other, own, ALU.is_gt)
            link(tt(tgg(oh2), other, own, ALU.is_equal))
            link(tt(tgg(oh2), tgg(oh2), lower[:, :, :].unsqueeze(1).to_broadcast([P, NT, NGROUPS, NGROUPS]),
                    ALU.mult))
            link(tt(oh1, oh1, oh2, ALU.add))
            rank = t5[:, 0:NT * NGROUPS]
            keep = t5[:, NT * NGROUPS:2 * NT * NGROUPS]
            penalty = t5[:, 2 * NT * NGROUPS:3 * NT * NGROUPS]
            link(V.tensor_reduce(rank, oh1.rearrange("p (n h) -> p n h", h=NGROUPS), AX_X, ALU.add))
            V.tensor_scalar(keep, rank, 1.5, None, ALU.is_lt)
            link(V.tensor_scalar(penalty, rank, 1.5, MASKED, ALU.is_ge, ALU.mult))

            def per_group(a):
                return a.unsqueeze(2).to_broadcast([P, NT * NGROUPS, GSIZE])

            def ns(a):
                return a.rearrange("p (n s) -> p n s", s=GSIZE)

            link(tt(ns(mk), ns(S), per_group(keep), ALU.mult))
            link(tt(ns(mk), ns(mk), per_group(penalty), ALU.add))

            def shared_hidden(g, blocks=range(IB)):
                for i in blocks:
                    dve.wait_ge(up_silu, g * IB + i + 1)
                    V.scalar_tensor_tensor(out=gs_of(g)[:, i, :], in0=psum[:, UP_BANKS[g * IB + i] + 1, :],
                                           scalar=sb12_sb[:, 1, i:i + 1], in1=gs_of(g)[:, i, :],
                                           op0=ALU.add, op1=ALU.mult).then_inc(up_ready, 1)

            for k, oh in enumerate((oh1, oh2)):
                link(V.tensor_reduce(tops[:, k, :], te(mk), AX_X, ALU.max))
                link(tt(te(cc), te(mk), over_e(tops[:, k, :]), ALU.is_equal))
                link(tt(te(cc), te(cc), over_t(rev_e[:, :]), ALU.mult))
                link(V.tensor_reduce(small[:, 0, :], te(cc), AX_X, ALU.max))
                link(tt(te(oh), te(cc), over_e(small[:, 0, :]), ALU.is_equal))
                if k == 0:
                    link(V.scalar_tensor_tensor(out=mk, in0=oh, scalar=TAKEN, in1=mk, op0=ALU.mult, op1=ALU.add))
            tt(chosen, oh1, oh2, ALU.add).then_inc(chosen_ready, 1)
            shared_hidden(0, [0])
            V.memset(gate17[:, :, E:E + 1], 1.0)
            tt(te(S), te(oh1), over_e(tops[:, 0, :]), ALU.mult)
            link(tt(te(cc), te(oh2), over_e(tops[:, 1, :]), ALU.mult))
            tt(gate17[:, :, 0:E], te(S), te(cc), ALU.add).then_inc(gates_ready, 1)

            shared_hidden(0, [1])

            dve.wait_ge(ranks_done, 1)
            tot, incl, excl = S, mk, cc
            cnt, ntile, end, base = (count[:, q, :] for q in range(4))

            def et(a):
                return a.rearrange("p (e t) -> p e t", t=NT)

            dve.wait_ge(gates_ready, 1)
            link(V.tensor_copy(et(tot), te(psum[:, 5, NT * E:2 * NT * E]).rearrange("p t e -> p e t")))
            link(V.tensor_copy(et(t5), restart[:, :].unsqueeze(1).to_broadcast([P, E, NT])))
            link(V.tensor_tensor_scan(incl, t5, tot, 0.0, ALU.mult, ALU.add))
            tt(excl, incl, tot, ALU.subtract)
            link(V.tensor_copy(cnt, et(incl)[:, :, NT - 1]))
            link(tt(et(t5), cnt.unsqueeze(2).to_broadcast([P, E, NT]),
                    steps128[:, :].unsqueeze(1).to_broadcast([P, E, NT]), ALU.is_gt))
            link(V.tensor_reduce(ntile, et(t5), AX_X, ALU.add))
            link(V.memset(small[:, 2, :], 1.0))
            link(V.tensor_tensor_scan(end, small[:, 2, :], ntile, 0.0, ALU.mult, ALU.add))
            link(tt(base, end, ntile, ALU.subtract))
            link(V.tensor_scalar(base, base, float(P), None, ALU.mult))
            tt(te(S), te(psum[:, 5, 0:NT * E]), et(excl).rearrange("p e t -> p t e"), ALU.add
               ).then_inc(ranks_read, 1)
            dve.wait_ge(ranks_read, 1)
            link(tt(te(S), te(S), over_t(base), ALU.add))
            for k, oh in enumerate((oh1, oh2)):
                link(tt(mk, oh, S, ALU.mult))
                link(V.tensor_reduce(pos[:, k, :], te(mk), AX_X, ALU.add))
            link(V.tensor_copy(pos_i[:, :, :], pos[:, :, :]))
            link(V.tensor_scalar(pos_i[:, :, :], pos_i[:, :, :], 7, None, ALU.arith_shift_right))
            link(V.tensor_copy(ptile[:, :, :], pos_i[:, :, :]))
            V.scalar_tensor_tensor(out=pslot[:, :, :], in0=ptile[:, :, :], scalar=-float(P),
                                   in1=pos[:, :, :], op0=ALU.mult, op1=ALU.add).then_inc(pslot_ready, 1)
            dve.wait_ge(pslot_ready, 1)
            J = TOPK * NT
            pt = ptile[:, :, :].rearrange("p k t -> p (k t)")
            pp = pslot[:, :, :].rearrange("p k t -> p (k t)")
            shared_hidden(1)
            dve.wait_ge(slots_ready, 1)
            dve.wait_ge(gateT_done, NG)
            JD = J - J_ACT
            tt(onehot_slot[:, 0:JD], slot_iota.unsqueeze(1).to_broadcast([P, JD, P]),
               pp[:, 0:JD].unsqueeze(2).to_broadcast([P, JD, P]), ALU.is_equal)
            link(tt(tile_code[:, :, 0, :], tile_iota[:, :].unsqueeze(1).to_broadcast([P, J, TW]),
                    pt.unsqueeze(2).to_broadcast([P, J, TW]), ALU.is_equal))
            V.tensor_scalar(tile_code[:, :, 1, :], tile_code[:, :, 0, :], part_iota[:, :], None, ALU.mult
                            ).then_inc(code_base_ready, 1)
            dve.wait_ge(code_base_ready, 1)
            tt(tile_code[:, 0:J_DVE, 0, :], tile_code[:, 0:J_DVE, 0, :],
               hi_code[:, 0:J_DVE].unsqueeze(2).to_broadcast([P, J_DVE, TW]), ALU.mult).then_inc(codes_ready, 1)

            def shared_sum(g, tiles=range(GT)):
                if g >= EARLY:
                    dve.wait_ge(x_again_loaded, 16 * (NT - EARLY * GT))
                for t in (g * GT + u for u in tiles):
                    dve.wait_ge(down_done, t + 1)
                    tt(acc_tile(t), acc_tile(t), psum[:, DOWN_BANKS[t], :], ALU.add).then_inc(z_ready, 1)

            shared_sum(0, range(2))
            dve.wait_ge(dispatch_done, 1)
            link(V.tensor_scalar(code_f[:, :], psum[:, 1, 0:TW], -float(P), float(ASSIGN), ALU.mult, ALU.add))
            link(tt(code_f[:, :], code_f[:, :], psum[:, 1, TW:2 * TW], ALU.add))
            link(V.tensor_copy(to_row[:, :], code_f[:, :]))
            V.tensor_scalar(from_row[:, 0:TW], to_row[:, :], TOKENS - 1, None, ALU.bitwise_and).then_inc(tables_ready, 1)
            shared_sum(0, range(2, GT))
            cmp = late_region[:, 2048:2048 + TW * E].rearrange("p (t e) -> p t e", e=E)
            link(tt(cmp, end.unsqueeze(1).to_broadcast([P, TW, E]),
                    tile_iota[:, :].unsqueeze(2).to_broadcast([P, TW, E]), ALU.is_le))
            link(V.tensor_reduce(code_f[:, :], cmp, AX_X, ALU.add))
            link(V.tensor_scalar(tile_expert[:, :], code_f[:, :], float(E - 1), float(HALF), ALU.min, ALU.add))
            link(V.tensor_scalar(tile_expert[:, :], tile_expert[:, :], E - 1, None, ALU.bitwise_and))
            n_pairs = tile_counts[:, N_PAIRS:N_PAIRS + 1]
            half = tile_counts[:, N_SCATTERED:N_SCATTERED + RING]
            link(V.tensor_scalar(n_pairs, end[:, E - 1:E], 1.0, None, ALU.add))
            link(V.tensor_scalar(n_pairs, n_pairs, 1, None, ALU.arith_shift_right))
            V.tensor_scalar(tile_counts[:, N_TILES:N_TILES + 1], n_pairs, 2.0, None, ALU.mult)
            V.tensor_scalar(tile_counts[:, N_TILES_LESS_2:N_TILES_LESS_2 + 1], n_pairs, 2.0, -2.0, ALU.mult, ALU.add)
            link(tt(half, n_pairs.to_broadcast([P, RING]), round_up[:, :], ALU.add))
            link(V.tensor_scalar(half, half, 1, None, ALU.arith_shift_right))
            V.scalar_tensor_tensor(out=half, in0=half, scalar=16.0, in1=last_slot[:, :],
                                   op0=ALU.mult, op1=ALU.add).then_inc(counts_ready, 1)
            shared_sum(1, range(GT - 1))

            def rows_transposed(b, done):
                dve.wait_ge(xgT_done, done)
                V.tensor_copy(xgT[:, b], psum[:, b, :].rearrange("p (c n) -> p c n", c=C)).then_inc(xgT_ready, 1)

            def dve_step(i, b):
                e = dve.value_load(tile_expert[0:1, bass.ds(i, 1)], min_val=0, max_val=E - 1)
                dve.wait_ge(h_done, i + 1)
                tt(h_sb[:, b], psum[:, 2 + b, 0:2 * INTER].rearrange("p (w n) -> p w n", w=2),
                   ebias[:, bass.ds(e, 1), :, :].rearrange("p u w n -> p (u w) n"), ALU.add).then_inc(h_ready, 1)
                rows_transposed(b, i + 3)
                dve.wait_ge(s_ready, i + 1)
                tt(g_sb[:, b, :], s_sb[:, b, :], h_sb[:, b, 1, :], ALU.mult).then_inc(g_ready, 1)

            def dve_pair(p):
                dve_step(p * 2, 0)
                dve_step(p * 2 + 1, 1)

            dve.wait_ge(half_loaded[0], 16 * (HALF + 1))
            dve.wait_ge(counts_ready, 1)
            rows_transposed(0, 1)
            shared_sum(1, [GT - 1])
            rows_transposed(1, 2)
            with dve.Fori(0, SURE) as p:
                dve_pair(p)
            pairs = count_of(dve, N_PAIRS)
            for p in (SURE, SURE + 1):
                with dve.If(pairs > p):
                    dve_pair(p)
            with dve.If(pairs > SURE + 2):
                with dve.Fori(SURE + 2, PAIRS) as p:
                    with dve.If(pairs > p):
                        dve_pair(p)

            def add_rows(g):
                dve.wait_ge(rows_loaded[g], 16 * TOPK)
                if g < EARLY:
                    dve.wait_ge(z_ready, (g + 1) * GT)
                else:
                    dve.wait_ge(x_again_loaded, 16 * (NT - EARLY * GT))
                ks = range(TOPK) if g < LAST else [0]
                for k in ks:
                    for t in range(g * GT, (g + 1) * GT):
                        if g == LAST:
                            dve.wait_ge(last_added, t % GT + 1)
                        ins = V.scalar_tensor_tensor(out=acc_tile(t), in0=rows_k[:, g, k, t % GT, :],
                                                     scalar=tops[:, k, t:t + 1], in1=acc_tile(t),
                                                     op0=ALU.mult, op1=ALU.add)
                        if k == TOPK - 1 and g < EARLY:
                            ins.then_inc(out_ready, 1)
                    if k < ks[-1] or g >= EARLY:
                        link(ins)

            shared_hidden(2)
            add_rows(0)
            add_rows(1)
            shared_hidden(3)
            add_rows(2)
            shared_sum(2)
            add_rows(3)
            shared_sum(3)


def kernel(**inputs):
    import numpy as np
    import concourse.bacc as bacc
    from concourse.bass_utils import run_bass_kernel_spmd

    nc = bacc.Bacc("TRN2", target_bir_lowering=False, num_devices=1)
    a = {n.removeprefix("L0_").removeprefix("cond_"): np.asarray(v) for n, v in inputs.items()}
    cond, b2 = np.asarray(inputs["cond_128"]), a["b2"]
    _, out_c, in_c, _ = a["weight"].shape
    chunks, dim = a["ffn_router_w"].shape[0] // P, a["ffn_router_w"].shape[0]
    experts = a["ffn_ew1"].shape[0]

    def rows(w):
        return w.reshape(-1, P, w.shape[-1]).transpose(1, 0, 2).reshape(P, -1)

    def in_places(w):
        return np.roll(w, experts // 2, axis=0)

    def everywhere(v):
        return np.broadcast_to(v, (P, v.size))

    mix = np.concatenate([a["weight"][..., 0].transpose(2, 0, 1), a["bias_k"].T[:, :, None]], axis=2)
    blocks = P // out_c
    by_place = cond.reshape(-1, blocks, cond.shape[1]).transpose(1, 0, 2).reshape(cond.shape)
    arrays = {
        "x": a["x"],
        "cond_pack": np.concatenate([by_place.T, a["W0"], a["W1"], a["W2"], a["b0"][:, None], a["b1"][:, None],
                                     everywhere(b2), np.tile(mix.reshape(in_c, -1), (blocks, 1))], axis=1),
        "router_pack": np.concatenate([rows(a["ffn_router_w"]), everywhere(a["ffn_router_b"]),
                                       everywhere(a["ffn_router_bias"]), rows(a["ffn_sb1"][:, None]),
                                       rows(a["ffn_sb2"][:, None])], axis=1),
        "shared_pack": np.concatenate([rows(a["ffn_sw1"]), rows(a["ffn_sw2"]), rows(a["ffn_sw3"])], axis=1),
        "expert_pack": in_places(np.concatenate(
            [a[w].reshape(experts, -1, P, a[w].shape[2]).transpose(0, 2, 1, 3).reshape(experts, P, -1)
             for w in ("ffn_ew1", "ffn_ew2", "ffn_ew3")], axis=2)),
        "expert_bias": in_places(np.concatenate([a["ffn_eb1"], a["ffn_eb2"]], axis=1)).reshape(1, -1),
        "down_bias": np.tile(np.concatenate([a["ffn_eb3"], a["ffn_sb3"][None, :]], axis=0), (6, 1)),
    }
    arrays = {n: np.ascontiguousarray(v) for n, v in arrays.items()}
    args = [nc.dram_tensor(n, v.shape, mybir.dt.from_np(v.dtype), kind="ExternalInput").ap()
            for n, v in arrays.items()]
    shape = inputs['x'].shape
    args.append(nc.dram_tensor("out_dram", shape, F32, kind="ExternalOutput").ap())
    adaln_moe_ffn(nc, *args)
    r = run_bass_kernel_spmd(nc, [arrays], core_ids=[0])
    return r.results[0]["out_dram"]
```
